# Optimizing a Trainium2 kernel written in Bass

```python
import numpy as np
import jax
import jax.numpy as jnp

def _softmax(x, axis=-1):
    return jax.nn.softmax(x, axis=axis)

def _gelu(x):
    return jax.nn.gelu(x, approximate=True)

def _silu(x):
    return jax.nn.silu(x)

def _sigmoid(x):
    return jax.nn.sigmoid(x)

def _layernorm(x, axis=-1, eps=1e-05):
    m = jnp.mean(x, axis=axis, keepdims=True)
    v = jnp.var(x, axis=axis, keepdims=True)
    return (x - m) / jnp.sqrt(v + eps)

def _scatter_add(tgt, idx, src, axis=0):
    return tgt.at[idx].add(src)

def _segment_sum(src, seg, n):
    return jax.ops.segment_sum(src, seg, n)
kernel_name = 'mk_conv_seq_d2_conv_nchw512_r2_c2f2f8'

def setup_inputs(seed: int=0):
    np.random.seed(seed)
    _w = jnp.asarray

    def _rec_inputs():
        import jax
        import jax.numpy as jnp
        _gk = jax.random.key(seed)
        x = -0.0002928 + 1 * jax.random.normal(jax.random.fold_in(_gk, 1), (8, 256, 32, 32), jnp.float32)
        return x
    x = _rec_inputs()

    def _L0_conv_setup():
        import jax, jax.numpy as jnp
        import numpy as np
        NUM_HEADS = 8
        NUM_GROUPS = 32
        EPS = 1e-05
        key = jax.random.key(seed)
        ks = jax.random.split(key, 7)
        B, C, Hs, Ws = (8, 256, 32, 32)
        x = jax.random.normal(ks[0], (B, C, Hs, Ws), jnp.float32)
        gn_w = 1.0 + 0.02 * jax.random.normal(ks[1], (C,), jnp.float32)
        gn_b = 0.02 * jax.random.normal(ks[2], (C,), jnp.float32)
        qkv_w = 0.02 * jax.random.normal(ks[3], (3 * C, C), jnp.float32)
        qkv_b = 0.02 * jax.random.normal(ks[4], (3 * C,), jnp.float32)
        proj_w = 0.02 * jax.random.normal(ks[5], (C, C), jnp.float32)
        proj_b = 0.02 * jax.random.normal(ks[6], (C,), jnp.float32)
        return {'x': x, 'gn_w': gn_w, 'gn_b': gn_b, 'qkv_w': qkv_w, 'qkv_b': qkv_b, 'proj_w': proj_w, 'proj_b': proj_b}
    _L0_conv_all = _L0_conv_setup()
    _L0_conv_in = {k: v for k, v in _L0_conv_all.items() if k in ('gn_w', 'gn_b', 'qkv_w', 'qkv_b', 'proj_w', 'proj_b')}
    del _L0_conv_all

    def _L1_conv_setup():
        import jax, jax.numpy as jnp
        import numpy as np
        key = jax.random.key(seed)
        k1, k2, k3, k4, k5 = jax.random.split(key, 5)
        B, C, H, W = (4, 256, 32, 32)
        Cq = C // 8
        x = jax.random.normal(k1, (B, C, H, W), dtype=jnp.float32)
        Wq = jax.random.normal(k2, (Cq, C), dtype=jnp.float32) * (1.0 / np.sqrt(C))
        Wk = jax.random.normal(k3, (Cq, C), dtype=jnp.float32) * (1.0 / np.sqrt(C))
        Wv = jax.random.normal(k4, (C, C), dtype=jnp.float32) * (1.0 / np.sqrt(C))
        gamma = jax.random.normal(k5, (1,), dtype=jnp.float32) * 0.1
        return {'x': x, 'Wq': Wq, 'Wk': Wk, 'Wv': Wv, 'gamma': gamma}
    _L1_conv_all = _L1_conv_setup()
    _L1_conv_in = {k: v for k, v in _L1_conv_all.items() if k in ('Wq', 'Wk', 'Wv', 'gamma')}
    del _L1_conv_all
    return {'x': x, 'L0_conv_gn_w': _L0_conv_in['gn_w'], 'L0_conv_gn_b': _L0_conv_in['gn_b'], 'L0_conv_qkv_w': _L0_conv_in['qkv_w'], 'L0_conv_qkv_b': _L0_conv_in['qkv_b'], 'L0_conv_proj_w': _L0_conv_in['proj_w'], 'L0_conv_proj_b': _L0_conv_in['proj_b'], 'L1_conv_Wq': _L1_conv_in['Wq'], 'L1_conv_Wk': _L1_conv_in['Wk'], 'L1_conv_Wv': _L1_conv_in['Wv'], 'L1_conv_gamma': _L1_conv_in['gamma']}

def reference(x, L0_conv_gn_w, L0_conv_gn_b, L0_conv_qkv_w, L0_conv_qkv_b, L0_conv_proj_w, L0_conv_proj_b, L1_conv_Wq, L1_conv_Wk, L1_conv_Wv, L1_conv_gamma):
    import jax
    import jax.numpy as jnp

    def _L0_conv_ref(x, gn_w, gn_b, qkv_w, qkv_b, proj_w, proj_b):
        import jax, jax.numpy as jnp
        import numpy as np
        NUM_HEADS = 8
        NUM_GROUPS = 32
        EPS = 1e-05
        B, C = (x.shape[0], x.shape[1])
        T = int(np.prod(x.shape[2:]))
        xr = x.reshape(B, C, T)
        g = xr.reshape(B, NUM_GROUPS, -1)
        mu = g.mean(axis=-1, keepdims=True)
        var = g.var(axis=-1, keepdims=True)
        h = ((g - mu) * jax.lax.rsqrt(var + EPS)).reshape(B, C, T)
        h = h * gn_w[:, None] + gn_b[:, None]
        qkv = jnp.einsum('oc,bct->bot', qkv_w, h) + qkv_b[:, None]
        ch = C // NUM_HEADS
        qkv = qkv.reshape(B * NUM_HEADS, 3 * ch, T)
        q, k, v = (qkv[:, :ch], qkv[:, ch:2 * ch], qkv[:, 2 * ch:])
        scale = 1.0 / jnp.sqrt(jnp.sqrt(jnp.asarray(ch, q.dtype)))
        w = jnp.einsum('bct,bcs->bts', q * scale, k * scale)
        w = jax.nn.softmax(w.astype(jnp.float32), axis=-1).astype(q.dtype)
        a = jnp.einsum('bts,bcs->bct', w, v).reshape(B, C, T)
        out = jnp.einsum('oc,bct->bot', proj_w, a) + proj_b[:, None]
        return (xr + out).reshape(x.shape)

    def _L1_conv_ref(x, Wq, Wk, Wv, gamma):
        import jax, jax.numpy as jnp
        import numpy as np
        b, c, h, w = x.shape
        n = h * w
        xf = x.reshape(b, c, n)
        q = jnp.einsum('oc,bcn->bno', Wq, xf)
        k = jnp.einsum('oc,bcn->bon', Wk, xf)
        v = jnp.einsum('oc,bcn->bon', Wv, xf)
        energy = jnp.einsum('bno,bom->bnm', q, k)
        attn = jax.nn.softmax(energy, axis=-1)
        out = jnp.einsum('bcj,bij->bci', v, attn)
        out = out.reshape(b, c, h, w)
        return gamma.reshape(()) * out + x

    def _gn(v, G=32, eps=1e-05):
        B_, C_, H_, W_ = v.shape
        g = v.reshape(B_, G, C_ // G, H_, W_)
        m = jnp.mean(g, axis=(2, 3, 4), keepdims=True)
        s = jnp.var(g, axis=(2, 3, 4), keepdims=True)
        return ((g - m) / jnp.sqrt(s + eps)).reshape(v.shape)

    def _ln_c(v, eps=1e-06):
        m = jnp.mean(v, axis=1, keepdims=True)
        s = jnp.var(v, axis=1, keepdims=True)
        return (v - m) / jnp.sqrt(s + eps)

    def _ln_t(v, eps=1e-05):
        m = jnp.mean(v, axis=-1, keepdims=True)
        s = jnp.var(v, axis=-1, keepdims=True)
        return (v - m) / jnp.sqrt(s + eps)

    def _to_tokens(v):
        B_, C_, H_, W_ = v.shape
        return v.reshape(B_, C_, H_ * W_).transpose(0, 2, 1)

    def _from_tokens(t, like):
        B_, C_, H_, W_ = like.shape
        return t.transpose(0, 2, 1).reshape(B_, C_, H_, W_)
    x = _L0_conv_ref(x, L0_conv_gn_w, L0_conv_gn_b, L0_conv_qkv_w, L0_conv_qkv_b, L0_conv_proj_w, L0_conv_proj_b)
    x = _L1_conv_ref(x, L1_conv_Wq, L1_conv_Wk, L1_conv_Wv, L1_conv_gamma)
    return x

_drawn_inputs = setup_inputs


def setup_inputs(seed=0):
    import zlib

    import numpy as np

    out = dict(_drawn_inputs(seed))
    spreads = {}
    factors = {'L0_conv_gn_w': 8.0,
     'L0_conv_gn_b': 8.0,
     'L0_conv_qkv_w': 8.0,
     'L0_conv_qkv_b': 8.0,
     'L0_conv_proj_w': 7.49,
     'L0_conv_proj_b': 49.869}
    for name, (base, spread) in spreads.items():
        noise = np.random.default_rng([zlib.crc32(name.encode()), seed]).standard_normal(out[name].shape)
        drawn = base * np.exp(spread * noise) if base else spread * noise
        out[name] = jnp.asarray(drawn.astype(out[name].dtype))
    for name, factor in factors.items():
        out[name] = (out[name] * factor).astype(out[name].dtype)
    return out
```

```python
from contextlib import ExitStack

import concourse.bass as bass
from concourse import mybir

F32 = mybir.dt.float32
F32R = mybir.dt.float32r
I32 = mybir.dt.int32
ACT = mybir.ActivationFunctionType
ALU = mybir.AluOpType
AX = mybir.AxisListType

P = 128
B, C, T = 8, 256, 1024
KT = C // P
HEADS, CH = 8, 32
GROUPS = 2
GH = HEADS // GROUPS
HALF = T // 2
SB = T // P
QUARTER = T // 4
EPS = 1e-5
NEWTON = 4
SCALE = float(CH) ** -0.25
HI_HI_LO = 3 * CH
ROWS = HI_HI_LO + 2
L0_UNITS, L1_UNITS = 64, 8
SLOTS = L0_UNITS + L1_UNITS
STACK_DMAS = 6 * GH
PRING = 4


def spread(plan, slot, rate, entries):
    for i, e in enumerate(entries):
        plan[slot + i // rate].append(e)


def max_entries(g, c):
    return [("M", g, c, j, tb, h) for j in range(GH) for tb in range(4) for h in range(2)] + [("MC", g, c)]


def plan_of(kind):
    plan = [[] for _ in range(SLOTS + 6)]
    before, after = kind != "first", kind in ("first", "steady")
    if kind == "prologue":
        plan[0] = [("PB",), ("STATS",), ("G1",), ("G2",)]
        plan[1] = [("QK", t, 0, n) for t in range(2) for n in range(2)]
        plan[2] = [("VT", 0, q) for q in range(2)]
        plan[3] = [("QK", t, 1, n) for t in range(2) for n in range(2)]
        plan[4] = max_entries(0, 0) + [("T", 0, 0)]
        return plan
    if kind == "epilogue":
        plan[0] = [("SUM", 1, 1)]
        plan[1] = [("P", m, n) for n in range(2) for m in range(KT)]
        plan[2] = [("QK1", n) for n in range(2)] + [("VT1", q) for q in range(4)]
        plan[3] = [("M1", tb, h) for tb in range(SB) for h in range(2)] + [("MC1",), ("T1",)]
        for c in range(4):
            spread(plan, 37 + 2 * c, 1, [("SUM1", c)])
        return plan
    spread(plan, 0, 1, [("VT", 1, q) for q in range(2)])
    spread(plan, 0, 3, max_entries(0, 1))
    if before:
        spread(plan, 2, 1, [("SUM", 1, 1)])
        spread(plan, 4, 2, [("P", m, n) for n in range(2) for m in range(KT)])
        spread(plan, 7, 2, [("QK1", n) for n in range(2)])
        spread(plan, 8, 2, [("VT1", q) for q in range(4)])
    spread(plan, 12, 1, [("T", 0, 1)])
    if after:
        spread(plan, 13, 1, [("STATS",), ("G1",), ("G2",)])
    spread(plan, 13, 3, max_entries(1, 0)[:24])
    spread(plan, 20, 1, [("SUM", 0, 0)])
    if before:
        spread(plan, 21, 3, [("M1", tb, h) for tb in range(SB) for h in range(2)] + [("MC1",)])
        spread(plan, 28, 1, [("T1",)])
    spread(plan, 27, 3, max_entries(1, 0)[24:])
    spread(plan, 31, 1, [("T", 1, 0)])
    if after:
        spread(plan, 32, 2, [("QK", t, 0, n) for t in range(2) for n in range(2)])
        spread(plan, 35, 1, [("VT", 0, q) for q in range(2)])
    spread(plan, 36, 1, [("SUM", 0, 1)])
    spread(plan, 33, 2, max_entries(1, 1))
    spread(plan, 51, 1, [("T", 1, 1)])
    if before:
        for c in range(4):
            spread(plan, 37 + 2 * c, 1, [("SUM1", c)])
    if after:
        spread(plan, 52, 1, [("QK", t, 1, n) for t in range(2) for n in range(2)])
        spread(plan, 53, 2, max_entries(0, 0))
        spread(plan, 72, 1, [("T", 0, 0)])
    spread(plan, 60, 1, [("SUM", 1, 0)])
    return plan


NO_BANK = ("MC", "MC1", "STATS")


def attention(nc, x, qkv_wT, qkv_b, gn_w, gn_b, proj_wT, proj_b, wqT, wkT, wvT, gamma, ident_in, gavg_in, out):
    x_v = x.rearrange("b (k p) t -> b p k t", p=P)
    out_v = out.rearrange("b (k p) t -> b p k t", p=P)

    kinds = ("prologue", "first", "steady", "last", "epilogue")
    plans = {k: plan_of(k) for k in kinds}
    banks = {k: [e for slot in plans[k] for e in slot if e[0] not in NO_BANK] for k in kinds}
    size = {k: len(banks[k]) for k in kinds}
    place = {k: {e: i for i, e in enumerate(banks[k])} for k in kinds}

    def w_base(kind, b):
        if kind == "prologue":
            return 0
        if kind == "first":
            return size["prologue"]
        steady = size["prologue"] + size["first"] - size["steady"]
        if kind == "epilogue":
            return steady + size["steady"] * (B - 1) + size["last"]
        return size["steady"] * b + steady

    with ExitStack() as ctx:
        def sb(name, shape, dt=F32):
            return ctx.enter_context(nc.sbuf_tensor(name, shape, dt))

        def sem(name):
            return ctx.enter_context(nc.semaphore(name))

        wqkv = sb("wqkv", [P, KT, 3 * C])
        wproj = sb("wproj", [P, KT, C])
        wqk1 = sb("wqk1", [P, KT, 2 * CH])
        wv1 = sb("wv1", [P, KT, C])
        qkvb = sb("qkvb", [P, 3 * KT])
        gnw = sb("gnw", [P, KT])
        gnb = sb("gnb", [P, KT])
        projb = sb("projb", [P, KT])
        outb = sb("outb", [P, KT])
        gam = sb("gam", [P, 1])
        ident = sb("ident", [P, P])
        gavg = sb("gavg", [P, P])
        ones = sb("ones", [P, P])
        xa = sb("xa", [P, KT, T])
        h = sb("h", [P, KT, T])
        y = sb("y", [P, KT, T])
        part_hi = sb("part_hi", [P, 2, T], F32R)
        part_lo = sb("part_lo", [P, 2, T])
        qs = [sb(f"qs{g}", [P, GH, T], F32R) for g in range(GROUPS)]
        ks = [sb(f"ks{g}", [P, GH, T], F32R) for g in range(GROUPS)]
        qs1 = sb("l1_qs", [P, T], F32R)
        ks1 = sb("l1_ks", [P, T], F32R)
        vt = sb("vt", [P, SB, C])
        vt1 = sb("l1_vt", [P, SB, C])
        probs = sb("probs", [P, PRING, T])
        acc = sb("acc", [P, 2, 2, T])
        acc1 = sb("acc1", [P, T])
        attn = sb("attn", [P, KT, T])
        raw1 = sb("raw1", [P, 4, KT, QUARTER])
        rec = sb("rec", [P, HALF])
        rec1 = sb("rec1", [P, QUARTER])
        bst = sb("bst", [P, KT, 2, 6])
        mv = sb("mv", [P, KT, 2])
        mu = sb("mu", [P, KT])
        dev = sb("dev", [P, KT])
        dev2 = sb("dev2", [P, KT])
        vpd = sb("vpd", [P, KT])
        rstd = sb("rstd", [P, KT])
        var = sb("var", [P, KT])
        half = sb("half", [P, KT], I32)
        aff_a = sb("aff_a", [P, KT])
        mua = sb("mua", [P, KT])
        aff_b = sb("aff_b", [P, KT])
        carry = sb("carry", [P, 1])
        mpart = sb("mpart", [P, 16, 2])
        mcol = sb("mcol", [P, 16])
        mpart1 = sb("mpart_l1", [P, SB, 2])
        mcol1 = sb("mcol_l1", [P, SB])
        mrow = [[sb(f"mrow{g}{c}", [16, 2, P], F32R) for c in range(2)] for g in range(GROUPS)]
        mrow1 = sb("mrow1", [SB, 2, P], F32R)

        st = ctx.enter_context(nc.psum_tensor("st", [P, 2, T], F32))
        work = ctx.enter_context(nc.psum_tensor("work", [P, 3, HALF], F32))
        pv = ctx.enter_context(nc.psum_tensor("pv", [P, HALF], F32))

        s_const = sem("s_const")
        s_ones = sem("s_ones")
        s_x = sem("s_x")
        s_y = sem("s_y")
        s_stats = sem("s_stats")
        s_rsqrt = sem("s_rsqrt")
        s_h = sem("s_h")
        s_w = sem("s_w")
        s_wd = sem("s_wd")
        s_t = sem("s_t")
        s_hi = sem("s_hi")
        s_hi1 = sem("s_hi1")
        s_stack = [sem(f"s_stack{g}") for g in range(GROUPS)]
        s_stack1 = sem("s_l1_stack")
        s_mc = [[sem(f"s_mc{g}{c}") for c in range(2)] for g in range(GROUPS)]
        s_mhi = [[sem(f"s_mhi{g}{c}") for c in range(2)] for g in range(GROUPS)]
        s_mrow = [[sem(f"s_mrow{g}{c}") for c in range(2)] for g in range(GROUPS)]
        s_mc1 = sem("s_mc1")
        s_mhi1 = sem("s_mhi1")
        s_mrow1 = sem("s_mrow1")
        s_st0 = sem("s_st0")
        s_st1 = sem("s_st1")
        s_exp0 = sem("s_exp0")
        s_exp1 = sem("s_exp1")
        s_pv0 = sem("s_pv0")
        s_pv1 = sem("s_pv1")
        s_copy0 = sem("s_copy0")
        s_copy1 = sem("s_copy1")
        s_add0 = sem("s_add0")
        s_add1 = sem("s_add1")
        s_rec = sem("s_rec")
        s_rec1 = sem("s_rec1")
        s_sc1 = sem("s_sc1")
        s_out = [sem(f"s_out{c}") for c in range(4)]

        ADDS0 = 14 * 4
        ADDS1 = 3 * 4

        def unit_use(n):
            if 32 <= n < 40:
                return 1, n - 32
            return 0, (n if n < 32 else n - L1_UNITS)

        def wait_unit_done(eng, sem0, sem1, n, b):
            layer, i = unit_use(n)
            if layer:
                eng.wait_ge(sem1, L1_UNITS * (b - 1) + i + 1)
            else:
                eng.wait_ge(sem0, L0_UNITS * b + i + 1)

        def slots_of(kind):
            if kind == "prologue":
                return []
            if kind == "epilogue":
                return list(range(32, 40))
            return [n for n in range(SLOTS) if kind != "first" or not 32 <= n < 40]

        def run_steps(eng, step):
            step("prologue", -1)
            step("first", 0)
            with eng.Fori(1, B - 1) as b:
                step("steady", b)
            step("last", B - 1)
            step("epilogue", B)

        block = ctx.enter_context(nc.Block())

        @block.sync
        def _(sp):
            for dst, src in ((wqkv[:, :, :], qkv_wT.rearrange("(k p) o -> p k o", p=P)),
                             (wproj[:, :, :], proj_wT.rearrange("(k p) o -> p k o", p=P)),
                             (wqk1[:, :, 0:CH], wqT.rearrange("(k p) o -> p k o", p=P)),
                             (wqk1[:, :, CH:2 * CH], wkT.rearrange("(k p) o -> p k o", p=P)),
                             (wv1[:, :, :], wvT.rearrange("(k p) o -> p k o", p=P)),
                             (qkvb[:, :], qkv_b), (gnw[:, :], gn_w), (gnb[:, :], gn_b), (projb[:, :], proj_b),
                             (gam[:, :], gamma), (ident[:, :], ident_in), (gavg[:, :], gavg_in)):
                sp.dma_start(dst, src).then_inc(s_const, 16)

            for c in range(4):
                sp.sem_inc(s_out[c], 16)

            def stack_group(g, kind, b):
                for t, stack in ((0, qs[g]), (1, ks[g])):
                    hi, lo = part_hi[:, t, :].bitcast(F32), part_lo[:, t, :]
                    rows = (hi, hi, lo) if t == 0 else (hi, lo, hi)
                    for r, src in enumerate(rows):
                        for j in range(GH):
                            sp.dma_start(stack[CH * r:CH * (r + 1), j, :].bitcast(F32),
                                         src[CH * j:CH * (j + 1), :]).then_inc(s_stack[g], 16)

            def max_rows(g, c, kind, b):
                sp.wait_ge(s_wd, w_base(kind, b) + place[kind][("T", g, c)] + 1)
                for part in range(2):
                    r = HI_HI_LO + part
                    for j in range(GH):
                        dst = qs[g][r:r + 1, j, c * HALF:(c + 1) * HALF].bitcast(F32).rearrange("o (t x) -> o t x", x=P)
                        sp.dma_start(dst, mrow[g][c][4 * j:4 * j + 4, part, :].bitcast(F32)).then_inc(s_mrow[g][c], 16)

            def step(kind, b):
                base = w_base(kind, b)
                wd = lambda e: base + place[kind][e] + 1
                if kind == "prologue":
                    sp.dma_start(xa[:, :, :], x_v[0]).then_inc(s_x, 16)
                    sp.wait_ge(s_wd, wd(("QK", 1, 0, 1)))
                    stack_group(0, kind, b)
                    max_rows(0, 0, kind, b)
                    return
                if kind != "epilogue":
                    sp.wait_ge(s_wd, base)
                    stack_group(1, kind, b)
                if kind in ("first", "steady"):
                    sp.wait_ge(s_h, b + 1)
                    sp.dma_start(xa[:, :, :], x_v[b + 1]).then_inc(s_x, 16)
                if kind == "first":
                    sp.dma_start(y[:, :, :], x_v[0]).then_inc(s_y, 16)
                if kind == "epilogue" or kind == "last" or kind == "steady":
                    sp.wait_ge(s_wd, wd(("QK1", 1)))
                    hi, lo = h[:, 0, :], h[:, 1, :]
                    for stack, p0, rows in ((qs1, 0, (hi, hi, lo)), (ks1, CH, (hi, lo, hi))):
                        for r, src in enumerate(rows):
                            sp.dma_start(stack[CH * r:CH * (r + 1), :].bitcast(F32), src[p0:p0 + CH, :]).then_inc(s_stack1, 16)
                if kind != "epilogue":
                    max_rows(0, 1, kind, b)
                if kind != "first":
                    sp.wait_ge(s_wd, wd(("T1",)))
                    for part in range(2):
                        r = HI_HI_LO + part
                        dst = qs1[r:r + 1, :].bitcast(F32).rearrange("o (t x) -> o t x", x=P)
                        sp.dma_start(dst, mrow1[:, part, :].bitcast(F32)).then_inc(s_mrow1, 16)
                if kind != "epilogue":
                    max_rows(1, 0, kind, b)
                if kind in ("first", "steady"):
                    sp.wait_ge(s_wd, wd(("QK", 1, 0, 1)))
                    stack_group(0, kind, b)
                if kind != "first":
                    for c in range(4):
                        sp.wait_ge(s_wd, wd(("SUM1", c)))
                        sp.dma_start(out_v[b - 1, :, :, c * QUARTER:(c + 1) * QUARTER],
                                     raw1[:, c, :, :]).then_inc(s_out[c], 16)
                if kind in ("steady", "last"):
                    sp.dma_start(y[:, :, :], x_v[b]).then_inc(s_y, 16)
                if kind != "epilogue":
                    max_rows(1, 1, kind, b)
                if kind in ("first", "steady"):
                    max_rows(0, 0, kind, b)

            run_steps(sp, step)
            for c in range(4):
                sp.wait_ge(s_out[c], 16 * (B + 1))

        @block.tensor
        def _(pe):
            mm = nc.tensor.matmul

            def scores_by_key(n, kind, b):
                layer, i = unit_use(n)
                if kind == "epilogue":
                    if n >= 34:
                        wait_unit_done(pe, s_exp0, s_exp1, n - 2, b)
                    elif n == 32:
                        pe.wait_ge(s_exp0, L0_UNITS * B)
                elif n >= 2:
                    before = n - 2
                    if kind == "first" and 32 <= before < 40:
                        before -= L1_UNITS
                    wait_unit_done(pe, s_exp0, s_exp1, before, b)
                elif kind != "first" and n == 0:
                    pe.wait_ge(s_exp0, L0_UNITS * b)
                if layer:
                    c, part = i // 2, i % 2
                    if i == 0:
                        pe.wait_ge(s_mrow1, 32 * b)
                    for q in range(4):
                        s0 = (4 * part + q) * P
                        last = mm(st[:, n % 2, q * QUARTER:(q + 1) * QUARTER], ks1[0:ROWS, s0:s0 + P],
                                  qs1[0:ROWS, c * QUARTER:(c + 1) * QUARTER], start=True, stop=True)
                    last.then_inc(s_st1, 1)
                    return
                g, c, blk, pair = i // 32, i // 16 % 2, i % 16 // 2, i % 2
                if i % 16 == 0:
                    pe.wait_ge(s_mrow[g][c], 128 * b + 128)
                for j in (2 * pair, 2 * pair + 1):
                    last = mm(st[:, n % 2, (j % 2) * HALF:(j % 2 + 1) * HALF], ks[g][0:ROWS, j, blk * P:(blk + 1) * P],
                              qs[g][0:ROWS, j, c * HALF:(c + 1) * HALF], start=True, stop=True)
                last.then_inc(s_st0, 1)

            def product_l0(n, b):
                _, i = unit_use(n)
                g, blk = i // 32, i % 16 // 2
                wait_unit_done(pe, s_exp0, s_exp1, n, b)
                for j in range(GH):
                    last = mm(pv[CH * j:CH * (j + 1), :], vt[:, blk, g * P + CH * j:g * P + CH * (j + 1)],
                              probs[:, (n - 1 + j // 2) % PRING, (j % 2) * HALF:(j % 2 + 1) * HALF],
                              start=(blk == 0), stop=(blk == SB - 1), tile_position=(0, CH * j))
                last.then_inc(s_pv0, 1)

            def pv_free(ci, kind, b):
                if ci == 0 and kind != "first":
                    pe.wait_ge(s_copy0, 4 * b)
                elif ci == 2 and kind != "first":
                    pe.wait_ge(s_copy1, 4 * b)
                elif ci > 0:
                    pe.wait_ge(s_copy0, 4 * b + ci)

            def product_l1(n, kind, b):
                _, i = unit_use(n)
                wait_unit_done(pe, s_exp0, s_exp1, n, b)
                if i == 0:
                    pe.wait_ge(s_copy0, 4 * B if kind == "epilogue" else 4 * b + 2)
                elif i % 2 == 0:
                    pe.wait_ge(s_copy1, 4 * (b - 1) + i // 2)
                for q in range(4):
                    for m in range(KT):
                        last = mm(pv[:, m * QUARTER:(m + 1) * QUARTER], vt1[:, 4 * (i % 2) + q, m * P:(m + 1) * P],
                                  probs[:, n % PRING, q * QUARTER:(q + 1) * QUARTER],
                                  start=(i % 2 == 0 and q == 0 and m == 0), stop=(i % 2 == 1 and q == 3),
                                  skip_group_check=True)
                last.then_inc(s_pv1, 1)

            def fill_bank(e, kind, b):
                base = w_base(kind, b)
                i = place[kind][e]
                wd = lambda x: base + place[kind][x] + 1
                if kind != "prologue" or i >= 3:
                    pe.wait_ge(s_wd, base + max(i - 2, 0))
                bank = work[:, i % 3, :]
                what = e[0]
                if what == "M":
                    _, g, c, j, tb, half = e
                    if (j, tb, half) == (0, 0, 0) and c == 0:
                        pe.wait_ge(s_stack[g], 16 * STACK_DMAS * (b + (2 if g == 0 else 1)))
                    t0 = c * HALF + tb * P
                    last = mm(bank, qs[g][0:HI_HI_LO, j, t0:t0 + P], ks[g][0:HI_HI_LO, j, half * HALF:(half + 1) * HALF],
                              start=True, stop=True)
                elif what == "M1":
                    _, tb, half = e
                    if (tb, half) == (0, 0):
                        pe.wait_ge(s_stack1, 96 * b)
                    last = mm(bank, qs1[0:HI_HI_LO, tb * P:(tb + 1) * P], ks1[0:HI_HI_LO, half * HALF:(half + 1) * HALF],
                              start=True, stop=True)
                elif what == "T":
                    _, g, c = e
                    pe.wait_ge(s_mc[g][c], b + (2 if (g, c) == (0, 0) else 1))
                    last = nc.tensor.transpose(bank[0:16, 0:P], mcol[:, :], ident[:, :])
                elif what == "T1":
                    pe.wait_ge(s_mc1, b)
                    last = nc.tensor.transpose(bank[0:SB, 0:P], mcol1[:, :], ident[:, :])
                elif what == "SUM":
                    _, g, c = e
                    n_acc = (4 * (b - 1) if (g, c) == (1, 1) else 4 * b) + 2 * g + c + 1
                    pe.wait_ge(s_add0, 14 * n_acc)
                    for j in range(GH):
                        last = mm(bank[CH * j:CH * (j + 1), :], ones[:, 0:CH],
                                  acc[:, c, j // 2, (j % 2) * HALF:(j % 2 + 1) * HALF], start=True, stop=True,
                                  tile_position=(0, CH * j))
                elif what == "SUM1":
                    pe.wait_ge(s_add1, ADDS1 * (b - 1) + 3 * (e[1] + 1))
                    last = mm(bank[:, 0:QUARTER], ones[:, :], acc1[:, 0:QUARTER], start=True, stop=True)
                elif what == "P":
                    _, m, n = e
                    if (m, n) == (0, 0):
                        pe.wait_ge(s_wd, wd(("SUM", 1, 1)))
                    for k in range(KT):
                        last = mm(bank, wproj[:, k, m * P:(m + 1) * P], attn[:, k, n * HALF:(n + 1) * HALF],
                                  start=(k == 0), stop=(k == KT - 1))
                elif what == "QK1":
                    n = e[1]
                    pe.wait_ge(s_wd, wd(("P", KT - 1, n)))
                    for k in range(KT):
                        last = mm(bank[0:2 * CH, :], wqk1[:, k, :], y[:, k, n * HALF:(n + 1) * HALF],
                                  start=(k == 0), stop=(k == KT - 1))
                elif what == "VT1":
                    for s in range(2):
                        blk = 2 * e[1] + s
                        for k in range(KT):
                            last = mm(bank[:, s * C:(s + 1) * C], y[:, k, blk * P:(blk + 1) * P], wv1[:, k, :],
                                      start=(k == 0), stop=(k == KT - 1))
                elif what == "PB":
                    pe.wait_ge(s_const, 16 * 12)
                    pe.wait_ge(s_ones, 4)
                    for m in range(KT):
                        for k in range(KT):
                            last = mm(bank[:, m:m + 1], wproj[:, k, m * P:(m + 1) * P], qkvb[:, 4 + k:5 + k],
                                      start=(k == 0), stop=(k == KT - 1))
                elif what == "G1":
                    pe.wait_ge(s_stats, 6 * (b + 1) + 1)
                    last = mm(bank[:, 0:KT], gavg[:, :], mv[:, :, 0], start=True, stop=True)
                elif what == "G2":
                    pe.wait_ge(s_wd, wd(("G1",)))
                    last = mm(bank[:, 0:KT], gavg[:, :], vpd[:, :], start=True, stop=True)
                elif what == "QK":
                    _, t, g, n = e
                    if (t, g, n) == (0, 0, 0):
                        pe.wait_ge(s_h, b + 2)
                    col = t * C + g * P
                    for k in range(KT):
                        last = mm(bank, wqkv[:, k, col:col + P], h[:, k, n * HALF:(n + 1) * HALF],
                                  start=(k == 0), stop=(k == KT - 1))
                elif what == "VT":
                    _, g, q = e
                    for s in range(4):
                        blk = 4 * q + s
                        for k in range(KT):
                            last = mm(bank[:, s * P:(s + 1) * P], h[:, k, blk * P:(blk + 1) * P],
                                      wqkv[:, k, 2 * C + g * P:2 * C + (g + 1) * P], start=(k == 0), stop=(k == KT - 1))
                last.then_inc(s_w, 1)

            def step(kind, b):
                units = slots_of(kind)
                base = w_base(kind, b)
                for n, entries in enumerate(plans[kind]):
                    if n in units:
                        scores_by_key(n, kind, b)
                    for e in entries:
                        if e[0] not in NO_BANK:
                            fill_bank(e, kind, b)
                    if 34 <= n < 42 and n - 2 in units:
                        if n == 34:
                            pe.wait_ge(s_wd, base + place[kind][("VT1", 3)] + 1)
                        product_l1(n - 2, kind, b)
                    if n % 2 and n - 3 in units and unit_use(n - 2)[0] == 0 and unit_use(n - 3)[0] == 0:
                        ci = unit_use(n - 2)[1] // 16
                        if unit_use(n - 2)[1] % 16 == 1:
                            pv_free(ci, kind, b)
                            if ci == 0:
                                pe.wait_ge(s_wd, base + place[kind][("VT", 1, 1)] + 1)
                        product_l0(n - 2, b)

            run_steps(pe, step)

        @block.scalar
        def _(act):
            def exponentials(n, kind, b):
                layer, i = unit_use(n)
                if layer:
                    act.wait_ge(s_st1, L1_UNITS * (b - 1) + i + 1)
                else:
                    act.wait_ge(s_st0, L0_UNITS * b + i + 1)
                prev = n - PRING
                if kind == "first" and 40 <= n < 44:
                    prev -= L1_UNITS
                if kind == "epilogue" and n < 32 + PRING:
                    if n == 32:
                        act.wait_ge(s_pv0, 32 * B)
                        act.wait_ge(s_add0, ADDS0 * B)
                elif prev >= 0:
                    pl, pi = unit_use(prev)
                    if pl:
                        act.wait_ge(s_pv1, L1_UNITS * (b - 1) + pi + 1)
                        act.wait_ge(s_add1, ADDS1 * (b - 1) + 3 * (pi // 2) + 1)
                    else:
                        act.wait_ge(s_pv0, 32 * b + pi // 2 + 1)
                        act.wait_ge(s_add0, ADDS0 * b + 14 * (pi // 16) + 2 * (max(pi % 16 // 2, 1) - 1) + pi % 2 + 1)
                elif kind != "first" and n == 0:
                    act.wait_ge(s_pv0, 32 * b)
                    act.wait_ge(s_add0, ADDS0 * b)
                nc.scalar.activation(probs[:, n % PRING, :], st[:, n % 2, :], ACT.Exp).then_inc(s_exp1 if layer else s_exp0, 1)

            def step(kind, b):
                if kind == "prologue":
                    return
                units = slots_of(kind)
                for n in range(SLOTS + 2):
                    if n in units:
                        exponentials(n, kind, b)
                    if 34 <= n < 42 and n % 2 and n - 2 in units:
                        c = (n - 35) // 2
                        act.wait_ge(s_pv1, L1_UNITS * (b - 1) + 2 * c + 2)
                        act.wait_ge(s_out[c], 16 * b)
                        nc.scalar.copy(raw1[:, c, :, :], pv[:, :].rearrange("p (m t) -> p m t", m=KT)).then_inc(s_copy1, 1)
                    if n in (17, 33, 57, 73) and kind != "epilogue":
                        ci = (17, 33, 57, 73).index(n)
                        act.wait_ge(s_pv0, 32 * b + 8 * (ci + 1))
                        if ci == 0 and kind != "first":
                            act.wait_ge(s_w, w_base(kind, b) + place[kind][("P", KT - 1, 1)] + 1)
                        nc.scalar.copy(attn[:, ci // 2, (ci % 2) * HALF:(ci % 2 + 1) * HALF], pv[:, :]).then_inc(s_copy0, 1)

            run_steps(act, step)

        @block.gpsimd
        def _(pool):
            pool.memset(ones[:, :], 1.0).then_inc(s_ones, 1)

            def step(kind, b):
                if kind == "prologue":
                    return
                base = w_base(kind, b)
                for n in slots_of(kind):
                    layer, i = unit_use(n)
                    if layer:
                        c = i // 2
                        if i % 2 == 0:
                            continue
                        pool.wait_ge(s_exp1, L1_UNITS * (b - 1) + i + 1)
                        if c:
                            pool.wait_ge(s_w, base + place[kind][("SUM1", c - 1)] + 1)
                        a0 = ADDS1 * (b - 1) + 3 * c
                        pool.tensor_tensor(acc1[:, :], probs[:, (n - 1) % PRING, :], probs[:, n % PRING, :],
                                           ALU.add).then_inc(s_add1, 1)
                        pool.wait_ge(s_add1, a0 + 1)
                        pool.tensor_tensor(acc1[:, 0:HALF], acc1[:, 0:HALF], acc1[:, HALF:T], ALU.add).then_inc(s_add1, 1)
                        pool.wait_ge(s_add1, a0 + 2)
                        pool.tensor_tensor(acc1[:, 0:QUARTER], acc1[:, 0:QUARTER], acc1[:, QUARTER:HALF],
                                           ALU.add).then_inc(s_add1, 1)
                        continue
                    ci, blk, pair = i // 16, i % 16 // 2, i % 2
                    if blk == 0:
                        continue
                    pool.wait_ge(s_exp0, L0_UNITS * b + i + 1)
                    if blk == 1 and pair == 0:
                        if ci == 0 and kind != "first":
                            pool.wait_ge(s_w, base)
                        elif ci == 1 and kind != "first":
                            pool.wait_ge(s_w, base + place[kind][("SUM", 1, 1)] + 1)
                        elif ci >= 2:
                            pool.wait_ge(s_w, base + place[kind][("SUM", 0, ci - 2)] + 1)
                    a = acc[:, ci % 2, pair, :]
                    if blk > 1:
                        pool.wait_ge(s_add0, ADDS0 * b + 14 * ci + 2 * (blk - 2) + pair + 1)
                    first = probs[:, (n - 2) % PRING, :] if blk == 1 else a
                    pool.tensor_tensor(a, first, probs[:, n % PRING, :], ALU.add).then_inc(s_add0, 1)

            run_steps(pool, step)

        @block.vector
        def _(dve):
            def use_bank(e, kind, b):
                base = w_base(kind, b)
                i = place[kind][e]
                dve.wait_ge(s_w, base + i + 1)
                bank = work[:, i % 3, :]
                what = e[0]
                if what == "M":
                    _, g, c, j, tb, half = e
                    last = dve.reduce_max(mpart[:, 4 * j + tb, half:half + 1], bank, AX.X)
                elif what == "M1":
                    _, tb, half = e
                    last = dve.reduce_max(mpart1[:, tb, half:half + 1], bank, AX.X)
                elif what in ("T", "T1"):
                    if what == "T":
                        _, g, c = e
                        ahead = 1 if (g, c) == (0, 0) else 0
                        rows, src, done, hi_done, n = (mrow[g][c], bank[0:16, 0:P], s_mrow[g][c], s_mhi[g][c], b + ahead)
                        if kind not in ("prologue", "first") or (kind == "first" and ahead):
                            dve.wait_ge(done, 128 * n)
                    else:
                        rows, src, hi_done, n = mrow1, bank[0:SB, 0:P], s_mhi1, b - 1
                    dve.tensor_scalar(rows[:, 0, :], src, -1.0, None, ALU.mult).then_inc(hi_done, 1)
                    dve.wait_ge(hi_done, n + 1)
                    last = dve.scalar_tensor_tensor(rows[:, 1, :], src, -1.0, rows[:, 0, :].bitcast(F32),
                                                    ALU.mult, ALU.subtract)
                elif what == "SUM":
                    _, g, c = e
                    ci = 2 * g + c
                    n = 4 * (b - 1 if ci == 3 else b) + ci
                    dve.reciprocal(rec[:, :], bank).then_inc(s_rec, 1)
                    dve.wait_ge(s_rec, n + 1)
                    dve.wait_ge(s_copy0, n + 1)
                    a = attn[:, g, c * HALF:(c + 1) * HALF]
                    last = dve.tensor_tensor(a, a, rec[:, :], ALU.mult)
                elif what == "SUM1":
                    c = e[1]
                    n = 4 * (b - 1) + c
                    dve.reciprocal(rec1[:, :], bank[:, 0:QUARTER]).then_inc(s_rec1, 1)
                    dve.wait_ge(s_rec1, n + 1)
                    dve.wait_ge(s_copy1, n + 1)
                    for m in range(KT):
                        dve.scalar_tensor_tensor(raw1[:, c, m, :], raw1[:, c, m, :], gam[:, 0:1], rec1[:, :],
                                                 ALU.mult, ALU.mult).then_inc(s_sc1, 1)
                    dve.wait_ge(s_sc1, 2 * n + 2)
                    last = dve.tensor_tensor(raw1[:, c, :, :], raw1[:, c, :, :], y[:, :, c * QUARTER:(c + 1) * QUARTER],
                                             ALU.add)
                elif what == "P":
                    _, m, n = e
                    if (m, n) == (0, 0):
                        dve.wait_ge(s_y, 16 * b)
                    yy = y[:, m, n * HALF:(n + 1) * HALF]
                    last = dve.scalar_tensor_tensor(yy, bank, outb[:, m:m + 1], yy, ALU.add, ALU.add)
                elif what == "QK1":
                    n = e[1]
                    src = bank[0:2 * CH, :]
                    hi = h[0:2 * CH, 0, n * HALF:(n + 1) * HALF]
                    dve.tensor_copy(hi.bitcast(F32R), src).then_inc(s_hi1, 1)
                    dve.wait_ge(s_hi1, 2 * (b - 1) + n + 1)
                    last = dve.tensor_tensor(h[0:2 * CH, 1, n * HALF:(n + 1) * HALF].bitcast(F32R), src, hi, ALU.subtract)
                elif what == "VT1":
                    last = dve.tensor_copy(vt1[:, 2 * e[1]:2 * e[1] + 2, :], bank.rearrange("p (s c) -> p s c", s=2))
                elif what == "PB":
                    last = dve.tensor_tensor(outb[:, :], bank[:, 0:KT], projb[:, :], ALU.add)
                elif what == "G1":
                    n = 6 * (b + 1)
                    dve.tensor_copy(mu[:, :], bank[:, 0:KT])
                    dve.tensor_tensor(dev[:, :], mv[:, :, 0], bank[:, 0:KT], ALU.subtract).then_inc(s_stats, 1)
                    dve.wait_ge(s_stats, n + 2)
                    dve.tensor_tensor(dev2[:, :], dev[:, :], dev[:, :], ALU.mult).then_inc(s_stats, 1)
                    dve.wait_ge(s_stats, n + 3)
                    last = dve.tensor_tensor(vpd[:, :], dev2[:, :], mv[:, :, 1], ALU.add)
                elif what == "G2":
                    last = dve.tensor_scalar(var[:, :], bank[:, 0:KT], EPS, None, ALU.add)
                elif what == "QK":
                    _, t, g, n = e
                    k = 8 * (b + 1) + 4 * g + 2 * t + n
                    if t == 0 and n == 0:
                        if g == 1:
                            dve.wait_ge(s_stack[0], 16 * STACK_DMAS * (b + 2))
                        elif kind != "prologue":
                            dve.wait_ge(s_stack[1], 16 * STACK_DMAS * (b + 1))
                    cols = slice(n * HALF, (n + 1) * HALF)
                    full, hi = part_lo[:, t, cols], part_hi[:, t, cols]
                    dve.tensor_scalar(full, bank, qkvb[:, 2 * t + g:2 * t + g + 1], SCALE, ALU.add,
                                      ALU.mult).then_inc(s_t, 1)
                    dve.wait_ge(s_t, k + 1)
                    dve.tensor_copy(hi, full).then_inc(s_hi, 1)
                    dve.wait_ge(s_hi, k + 1)
                    last = dve.tensor_tensor(full.bitcast(F32R), full, hi.bitcast(F32), ALU.subtract)
                elif what == "VT":
                    _, g, q = e
                    last = dve.tensor_copy(vt[:, 4 * q:4 * q + 4, g * P:(g + 1) * P], bank.rearrange("p (s c) -> p s c", s=4))
                last.then_inc(s_wd, 1)
                if what == "G2":
                    normalize(kind, b)

            def normalize(kind, b):
                base = w_base(kind, b)
                n = 6 * (b + 1)
                dve.wait_ge(s_wd, base + place[kind][("G2",)] + 1)
                k = (2 + 3 * NEWTON) * (b + 1)
                dve.tensor_scalar(half[:, :], var[:, :].bitcast(I32), 1, None, ALU.logical_shift_right).then_inc(s_rsqrt, 1)
                dve.wait_ge(s_rsqrt, k + 1)
                dve.tensor_scalar(rstd[:, :].bitcast(I32), half[:, :], -1.0, float(0x5F3759DF), ALU.mult,
                                  ALU.add).then_inc(s_rsqrt, 1)
                for i in range(NEWTON):
                    dve.wait_ge(s_rsqrt, k + 2 + 3 * i)
                    dve.scalar_tensor_tensor(dev[:, :], rstd[:, :], -0.5, rstd[:, :], ALU.mult, ALU.mult).then_inc(s_rsqrt, 1)
                    dve.wait_ge(s_rsqrt, k + 3 + 3 * i)
                    dve.tensor_tensor(dev2[:, :], dev[:, :], var[:, :], ALU.mult).then_inc(s_rsqrt, 1)
                    dve.wait_ge(s_rsqrt, k + 4 + 3 * i)
                    dve.scalar_tensor_tensor(rstd[:, :], dev2[:, :], 1.5, rstd[:, :], ALU.add, ALU.mult).then_inc(s_rsqrt, 1)
                dve.wait_ge(s_rsqrt, k + 2 + 3 * NEWTON)
                dve.tensor_tensor(aff_a[:, :], rstd[:, :], gnw[:, :], ALU.mult).then_inc(s_stats, 1)
                dve.wait_ge(s_stats, n + 4)
                dve.tensor_tensor(mua[:, :], mu[:, :], aff_a[:, :], ALU.mult).then_inc(s_stats, 1)
                dve.wait_ge(s_stats, n + 5)
                dve.tensor_tensor(aff_b[:, :], gnb[:, :], mua[:, :], ALU.subtract).then_inc(s_stats, 1)
                dve.wait_ge(s_stats, n + 6)
                if kind != "prologue":
                    dve.wait_ge(s_w, base + place[kind][("VT", 1, 1)] + 1)
                    if kind != "first":
                        dve.wait_ge(s_stack1, 96 * b)
                dve.tensor_scalar(h[:, 0, :], xa[:, 0, :], aff_a[:, 0:1], aff_b[:, 0:1], ALU.mult, ALU.add)
                dve.tensor_scalar(h[:, 1, :], xa[:, 1, :], aff_a[:, 1:2], aff_b[:, 1:2], ALU.mult,
                                  ALU.add).then_inc(s_h, 1)

            def own_step(e, kind, b):
                base = w_base(kind, b)
                if e[0] == "STATS":
                    dve.wait_ge(s_x, 16 * (b + 2))
                    for k in range(KT):
                        for n in range(2):
                            s = dve.bn_stats(bst[:, k, n, :], xa[:, k, n * HALF:(n + 1) * HALF])
                    s.then_inc(s_bn, 1)
                    dve.wait_ge(s_bn, b + 2)
                    dve.memset(carry[:, :], 0.0)
                    dve.bn_aggr(mv[:, 0, :], bst[:, 0, :, :])
                    dve.bn_aggr(mv[:, 1, :], bst[:, 1, :, :]).then_inc(s_stats, 1)
                elif e[0] == "MC":
                    _, g, c = e
                    dve.wait_ge(s_wd, base + place[kind][("M", g, c, GH - 1, 3, 1)] + 1)
                    dve.tensor_tensor(mcol[:, :], mpart[:, :, 0], mpart[:, :, 1], ALU.max).then_inc(s_mc[g][c], 1)
                else:
                    dve.wait_ge(s_wd, base + place[kind][("M1", SB - 1, 1)] + 1)
                    dve.tensor_tensor(mcol1[:, :], mpart1[:, :, 0], mpart1[:, :, 1], ALU.max).then_inc(s_mc1, 1)

            def step(kind, b):
                for entries in plans[kind]:
                    for e in entries:
                        if e[0] in NO_BANK:
                            own_step(e, kind, b)
                        else:
                            use_bank(e, kind, b)

            s_bn = sem("s_bn")
            for rows in (ks[0][HI_HI_LO:ROWS, :, :], ks[1][HI_HI_LO:ROWS, :, :], ks1[HI_HI_LO:ROWS, :]):
                dve.memset(rows.bitcast(F32), 1.0).then_inc(s_ones, 1)
            dve.wait_ge(s_const, 16 * 12)
            run_steps(dve, step)


def kernel(x, L0_conv_gn_w, L0_conv_gn_b, L0_conv_qkv_w, L0_conv_qkv_b, L0_conv_proj_w, L0_conv_proj_b,
           L1_conv_Wq, L1_conv_Wk, L1_conv_Wv, L1_conv_gamma):
    import numpy as np
    import concourse.bacc as bacc
    from concourse.bass_utils import run_bass_kernel_spmd

    def columns(v):
        return np.ascontiguousarray(np.asarray(v).reshape(-1, P).T)

    def parts_first(w):
        w = np.asarray(w)
        return np.swapaxes(w.reshape(HEADS, 3, CH, -1), 0, 1).reshape(3 * C, -1)

    x = np.asarray(x)
    group = np.arange(P) // (C // 32)
    arrays = {
        "x": np.ascontiguousarray(x.reshape(B, C, T)),
        "qkv_wT": np.ascontiguousarray(parts_first(L0_conv_qkv_w).T),
        "qkv_b": columns(parts_first(L0_conv_qkv_b).reshape(-1)),
        "gn_w": columns(L0_conv_gn_w),
        "gn_b": columns(L0_conv_gn_b),
        "proj_wT": np.ascontiguousarray(np.asarray(L0_conv_proj_w).T),
        "proj_b": columns(L0_conv_proj_b),
        "wqT": np.ascontiguousarray(np.asarray(L1_conv_Wq).T),
        "wkT": np.ascontiguousarray(np.asarray(L1_conv_Wk).T),
        "wvT": np.ascontiguousarray(np.asarray(L1_conv_Wv).T),
        "gamma": np.ascontiguousarray(np.broadcast_to(np.asarray(L1_conv_gamma).reshape(1, 1), (P, 1))),
        "ident": np.eye(P, dtype=np.float32),
        "gavg": ((group[:, None] == group[None, :]) / (C // 32)).astype(np.float32),
    }
    nc = bacc.Bacc("TRN2", target_bir_lowering=False, num_devices=1)
    args = [nc.dram_tensor(f"in_{k}", a.shape, mybir.dt.from_np(a.dtype), kind="ExternalInput").ap()
            for k, a in arrays.items()]
    out = nc.dram_tensor("out_0", (B, C, T), F32, kind="ExternalOutput").ap()
    attention(nc, *args, out)
    r = run_bass_kernel_spmd(nc, [{f"in_{k}": a for k, a in arrays.items()}], core_ids=[0])
    return r.results[0]["out_0"].reshape(x.shape)
```

```python
from contextlib import ExitStack

import concourse.bass as bass
from concourse import mybir

F32 = mybir.dt.float32
F32R = mybir.dt.float32r
I32 = mybir.dt.int32
ACT = mybir.ActivationFunctionType
ALU = mybir.AluOpType
AX = mybir.AxisListType

P = 128
B, C, T = 8, 256, 1024
KT = C // P
HEADS, CH = 8, 32
GROUPS = 2
GH = HEADS // GROUPS
HALF = T // 2
SB = T // P
QUARTER = T // 4
EPS = 1e-5
NEWTON = 3
SCALE = float(CH) ** -0.25
HI_HI_LO = 3 * CH
ROWS = HI_HI_LO + 2
L0_UNITS, L1_UNITS = 64, 8
SLOTS = L0_UNITS + L1_UNITS
STACK_DMAS = 6 * GH
PRING = 4
ST_BANKS, WORK_BANKS = 3, 4


L1_AT = 48
PIECES, PIECES1 = 4, 2
PIECE = HALF // PIECES

MAXIMA_OF_SLOT = (0, 3, 3, 2, 3, 1, 4, 1, 3, 1, 1, 3, 1, 2, 4, 2, 0, 1, 4, 0, 0, 1, 5, 1, 2, 3, 2, 5, 0, 3, 4, 0, 0, 1, 1, 0,
                  3, 1, 3, 2, 2, 2, 1, 4, 0, 2, 5, 1, 2, 1, 0, 3, 0, 4, 3, 1, 2, 2, 2, 0, 2, 0, 3, 6, 0, 0, 3, 1, 1, 1, 4, 2)
STEADY = {
    "maxima1": (19, 19, 24, 24, 26, 28, 28, 31, 32, 32, 33, 34, 34, 37, 38, 42, 43, 44),
    "last_block": (0, 16, 33, 50),
    "qk1": (59, 63, 67, 67, 67, 69),
    "norm": (9, 12, 13, 15, 17, 17, 19, 22, 24, 25, 34, 35),
    "sums": (3, 4, 5, 5, 6, 18, 20, 20, 21, 23, 35, 37, 38, 40, 40, 52, 52, 52, 60, 62),
    "sums1": (52, 54, 54, 54, 54, 55, 56, 57, 58, 58, 64, 65),
    "v0": (39, 40),
    "layer1": (0, 5, 10, 12, 15, 15, 27, 34, 38, 40),
    "split0": (34, 35),
    "v1": (6, 8),
    "maxima": [n for n, count in enumerate(MAXIMA_OF_SLOT) for _ in range(count)],
}
NORM_STEPS = [("BN", 0), ("BN", 1), ("AGG",), ("G1",), ("G2",), ("NORM",), ("H", 0), ("H", 1)]


def spread(plan, start, end, entries):
    for i, e in enumerate(entries):
        plan[start + i * (end - start) // len(entries)].append(e)


def max_entries(g, c):
    return [("M", g, c, j, tb, h) for j in range(GH) for tb in range(4) for h in range(2)] + [("MC", g, c), ("T", g, c)]


def plan_of(kind):
    plan = [[] for _ in range(SLOTS)]
    before, after = kind != "first", kind in ("first", "steady")
    chunk = {(g, c): max_entries(g, c) for g in range(GROUPS) for c in range(2)}
    maxima1 = [("M1", tb, h) for tb in range(SB) for h in range(2)] + [("MC1",), ("T1",)]
    qk = [[("QK", t, g, n) if n < 2 else ("HL", t, g) for t in range(2) for n in range(3)] for g in range(GROUPS)]
    early = 16

    def sums(g, c):
        return [("SUM", g, c)] + [("R", g, c, p) for p in range(PIECES)]

    def sums1(c):
        return [("SUM1", c)] + [("R1", c, p) for p in range(PIECES1)]

    if kind == "prologue":
        plan[0] = list(NORM_STEPS)
        plan[1] = qk[0]
        plan[2] = [e for e in qk[1] if e[0] == "QK"]
        plan[3] = chunk[0, 0] + [("HL", 0, 1), ("HL", 1, 1)]
        spread(plan, 4, 8, [("VT", 0, q) for q in range(2)] + [("PB",)])
        spread(plan, 4, 8, chunk[0, 1][:early])
        return plan
    if kind == "epilogue":
        plan[0].append(("A", 3))
        plan[2] += [("P", m, 0) for m in range(KT)] + [("QK1", 0), ("VT1", 0), ("VT1", 1)]
        plan[3] += sums(1, 1)
        plan[8] += [("P", m, 1) for m in range(KT)] + [("QK1", 1), ("VT1", 2), ("VT1", 3)] + maxima1
        for c in range(4):
            plan[L1_AT + 4 + 2 * c] += sums1(c)
        return plan
    maxima = chunk[0, 1][early:] + chunk[1, 0] + chunk[1, 1] + chunk[0, 0] + chunk[0, 1][:early]
    of_next = set(chunk[0, 0] + chunk[0, 1][:early])
    chains = {
        "last_block": [("A", ci) for ci in (3, 0, 1, 2)],
        "norm": NORM_STEPS + [e for e in qk[0] if e[0] == "QK"],
        "split0": [e for e in qk[0] if e[0] == "HL"],
        "sums": sums(1, 1) + sums(0, 0) + sums(0, 1) + sums(1, 0),
        "sums1": [e for c in range(4) for e in sums1(c)],
        "v1": [("VT", 1, q) for q in range(2)],
        "layer1": [("P", m, n) for n in range(2) for m in range(KT)] + [("QK1", n) for n in range(2)]
                  + [("VT1", q) for q in range(4)],
        "qk1": qk[1],
        "v0": [("VT", 0, q) for q in range(2)],
        "maxima1": maxima1,
        "maxima": maxima,
    }
    for name, slots in STEADY.items():
        for e, n in zip(chains[name], slots):
            of_before = name in ("sums1", "layer1", "maxima1") or e[:3] in (("SUM", 1, 1), ("R", 1, 1)) or e == ("A", 3)
            of_after = name in ("norm", "split0", "qk1", "v0") or (name == "maxima" and e in of_next)
            if (before or not of_before) and (after or not of_after):
                plan[n].append(e)
    return plan


NO_BANK = ("MC", "MC1", "BN", "AGG", "NORM", "H", "HL", "A", "R", "R1")
SCALAR_USES = ("QK", "VT", "VT1", "SUM", "SUM1")


def attention(nc, x, qkv_wT, qkv_b, gn_w, gn_b, proj_wT, proj_b, wqT, wkT, wvT, gamma, ident_in, gavg_in, out):
    x_v = x.rearrange("b (k p) t -> b p k t", p=P)
    out_v = out.rearrange("b (k p) t -> b p k t", p=P)

    kinds = ("prologue", "first", "steady", "last", "epilogue")
    plans = {k: plan_of(k) for k in kinds}
    banks = {k: [e for slot in plans[k] for e in slot if e[0] not in NO_BANK] for k in kinds}
    place = {k: {e: i for i, e in enumerate(banks[k])} for k in kinds}
    users = {"w": lambda e: True, "a": lambda e: e[0] in SCALAR_USES, "d": lambda e: e[0] not in SCALAR_USES}
    size = {u: {k: sum(map(of, banks[k])) for k in kinds} for u, of in users.items()}
    turn = {k: {e: sum(map(users["a" if e[0] in SCALAR_USES else "d"], banks[k][:i + 1]))
                for i, e in enumerate(banks[k])} for k in kinds}

    def w_base(kind, b, user="w"):
        n = size[user]
        if kind == "prologue":
            return 0
        if kind == "first":
            return n["prologue"]
        steady = n["prologue"] + n["first"] - n["steady"]
        if kind == "epilogue":
            return steady + n["steady"] * (B - 1) + n["last"]
        return n["steady"] * b + steady

    with ExitStack() as ctx:
        def sb(name, shape, dt=F32):
            return ctx.enter_context(nc.sbuf_tensor(name, shape, dt))

        def sem(name):
            return ctx.enter_context(nc.semaphore(name))

        wqkv = sb("wqkv", [P, KT, 3 * C])
        wproj = sb("wproj", [P, KT, C])
        wqk1 = sb("wqk1", [P, KT, 2 * CH])
        wv1 = sb("wv1", [P, KT, C])
        qkvb = sb("qkvb", [P, 3 * KT])
        qkbs = sb("qkbs", [P, 4])
        gnw = sb("gnw", [P, KT])
        gnb = sb("gnb", [P, KT])
        projb = sb("projb", [P, KT])
        outb = sb("outb", [P, KT])
        gam = sb("gam", [P, 1])
        ident = sb("ident", [P, P])
        gavg = sb("gavg", [P, P])
        ones = sb("ones", [P, P])
        xa = sb("xa", [P, KT, T])
        h = sb("h", [P, KT, T])
        y = sb("y", [P, KT, T])
        part_hi = sb("part_hi", [P, 2, T], F32R)
        part_lo = sb("part_lo", [P, 2, T])
        qs = [sb(f"qs{g}", [P, GH, T], F32R) for g in range(GROUPS)]
        ks = [sb(f"ks{g}", [P, GH, T], F32R) for g in range(GROUPS)]
        qs1 = sb("l1_qs", [P, T], F32R)
        ks1 = sb("l1_ks", [P, T], F32R)
        vt = sb("vt", [P, SB, C])
        vt1 = sb("l1_vt", [P, SB, C])
        probs = sb("probs", [P, PRING, T])
        acc = sb("acc", [P, 2, 2, T])
        attn = sb("attn", [P, KT, T])
        raw1 = sb("raw1", [P, 4, KT, QUARTER])
        rec = sb("rec", [P, HALF])
        rec1 = sb("rec1", [P, 2, QUARTER])
        acc1 = acc[:, 1, 0, :]
        bst = sb("bst", [P, KT, 2, 6])
        mv = sb("mv", [P, KT, 2])
        mu = sb("mu", [P, KT])
        dev = sb("dev", [P, KT])
        dev2 = sb("dev2", [P, KT])
        vpd = sb("vpd", [P, KT])
        rstd = sb("rstd", [P, KT])
        var = sb("var", [P, KT])
        half = sb("half", [P, KT], I32)
        aff_a = sb("aff_a", [P, KT])
        mua = sb("mua", [P, KT])
        aff_b = sb("aff_b", [P, KT])
        carry = sb("carry", [P, 1])
        mpart = sb("mpart", [P, 16, 2])
        mcol = sb("mcol", [P, 16])
        mpart1 = sb("mpart_l1", [P, SB, 2])
        mcol1 = sb("mcol_l1", [P, SB])
        mrow = [[sb(f"mrow{g}{c}", [16, 2, P], F32R) for c in range(2)] for g in range(GROUPS)]
        mrow1 = sb("mrow1", [SB, 2, P], F32R)

        st = ctx.enter_context(nc.psum_tensor("st", [P, ST_BANKS, HALF], F32))
        work = ctx.enter_context(nc.psum_tensor("work", [P, WORK_BANKS, HALF], F32))
        pv = ctx.enter_context(nc.psum_tensor("pv", [P, HALF], F32))

        s_norm_const = sem("s_norm_const")
        s_const = sem("s_const")
        s_ones = sem("s_ones")
        s_x = sem("s_x")
        s_y = sem("s_y")
        s_stats = sem("s_stats")
        s_rsqrt = sem("s_rsqrt")
        s_h = sem("s_h")
        s_w = sem("s_w")
        s_wd = sem("s_wd")
        s_wa = sem("s_wa")
        s_part = sem("s_part")
        s_scaled = sem("s_scaled")
        s_hi = sem("s_hi")
        s_hi1 = sem("s_hi1")
        s_stack = [sem(f"s_stack{g}") for g in range(GROUPS)]
        s_soft = sem("s_soft")
        s_stack1 = sem("s_l1_stack")
        s_mc = [[sem(f"s_mc{g}{c}") for c in range(2)] for g in range(GROUPS)]
        s_mhi = [[sem(f"s_mhi{g}{c}") for c in range(2)] for g in range(GROUPS)]
        s_mrow = [[sem(f"s_mrow{g}{c}") for c in range(2)] for g in range(GROUPS)]
        s_mc1 = sem("s_mc1")
        s_mhi1 = sem("s_mhi1")
        s_mrow1 = sem("s_mrow1")
        s_st0 = sem("s_st0")
        s_st1 = sem("s_st1")
        s_exp0 = sem("s_exp0")
        s_exp1 = sem("s_exp1")
        s_pv0 = sem("s_pv0")
        s_pv1 = sem("s_pv1")
        s_copy0 = sem("s_copy0")
        s_copy1 = sem("s_copy1")
        s_add0 = sem("s_add0")
        s_addv = sem("s_addv")
        s_add1 = sem("s_add1")
        s_rec = sem("s_rec")
        s_norm = sem("s_norm")
        s_done1 = sem("s_done1")
        s_rec1 = sem("s_rec1")
        s_sc1 = sem("s_sc1")
        s_out = [sem(f"s_out{c}") for c in range(4)]

        ADDS0 = 13 * 4
        ADDS1 = 3 * 4
        L1_CHUNK = L1_AT // 16

        def wait_used(eng, e, kind, b):
            if e[0] in SCALAR_USES:
                eng.wait_ge(s_wa, w_base(kind, b, "a") + turn[kind][e])
            else:
                eng.wait_ge(s_wd, w_base(kind, b, "d") + turn[kind][e])

        def unit_use(n):
            if L1_AT <= n < L1_AT + L1_UNITS:
                return 1, n - L1_AT
            return 0, (n if n < L1_AT else n - L1_UNITS)

        def wait_used_before(eng, bank, kind, b):
            kinds_before = {"first": ("prologue",), "steady": ("first", "steady"), "last": ("steady",), "epilogue": ("last",)}[kind]
            since = {}
            for k in kinds_before:
                e = banks[k][-1 - (len(banks[k]) - 1 - bank) % WORK_BANKS]
                user = "a" if e[0] in SCALAR_USES else "d"
                since[user] = min(since.get(user, 1 << 30), size[user][k] - turn[k][e])
            for user, n in since.items():
                eng.wait_ge(s_wa if user == "a" else s_wd, w_base(kind, b, user) - n)

        def wait_exp(eng, n, b, halves=2):
            layer, i = unit_use(n)
            if layer:
                eng.wait_ge(s_exp1, 2 * (L1_UNITS * (b - 1) + i) + halves)
            else:
                eng.wait_ge(s_exp0, 2 * (L0_UNITS * b + i) + halves)

        def wait_added(eng, i, b):
            ci, blk, pair = i // 16, i % 16 // 2, i % 2
            if blk == SB - 1 and pair == 1:
                eng.wait_ge(s_addv, 4 * b + ci + 1)
            else:
                eng.wait_ge(s_add0, ADDS0 * b + 13 * ci + 2 * (max(blk, 1) - 1) + pair + 1)

        def last_slot(ci):
            return 16 * ci + 15 + (L1_UNITS if ci >= L1_CHUNK else 0)

        def slots_of(kind):
            if kind == "prologue":
                return []
            if kind == "epilogue":
                return list(range(L1_AT, L1_AT + L1_UNITS))
            return [n for n in range(SLOTS) if kind != "first" or not L1_AT <= n < L1_AT + L1_UNITS]

        def stack_rows(eng, g, t, rows=(0, 1, 2), done=None):
            stack = (qs, ks)[t][g]
            hi, lo = part_hi[:, t, :].bitcast(F32), part_lo[:, t, :]
            for r in rows:
                src = ((hi, hi, lo) if t == 0 else (hi, lo, hi))[r]
                for j in range(GH):
                    eng.dma_start(stack[CH * r:CH * (r + 1), j, :].bitcast(F32),
                                  src[CH * j:CH * (j + 1), :]).then_inc(done or s_stack[g], 16)

        def run_steps(eng, step):
            step("prologue", -1)
            step("first", 0)
            with eng.Fori(1, B - 1) as b:
                step("steady", b)
            step("last", B - 1)
            step("epilogue", B)

        block = ctx.enter_context(nc.Block())

        @block.sync
        def _(sp):
            for k in range(KT):
                sp.dma_start(xa[:, k, :], x_v[0, :, k, :]).then_inc(s_x, 16)
            for dst, src in ((gavg[:, :], gavg_in), (gnw[:, :], gn_w), (gnb[:, :], gn_b), (qkvb[:, :], qkv_b)):
                sp.dma_start(dst, src).then_inc(s_norm_const, 16)
            for dst, src in ((wqkv[:, :, :], qkv_wT.rearrange("(k p) o -> p k o", p=P)),
                             (ident[:, :], ident_in),
                             (wproj[:, :, :], proj_wT.rearrange("(k p) o -> p k o", p=P)),
                             (wqk1[:, :, 0:CH], wqT.rearrange("(k p) o -> p k o", p=P)),
                             (wqk1[:, :, CH:2 * CH], wkT.rearrange("(k p) o -> p k o", p=P)),
                             (wv1[:, :, :], wvT.rearrange("(k p) o -> p k o", p=P)),
                             (projb[:, :], proj_b), (gam[:, :], gamma)):
                sp.dma_start(dst, src).then_inc(s_const, 16)
            for c in range(4):
                sp.sem_inc(s_out[c], 16)

            def max_rows(g, c, kind, b):
                wait_used(sp, ("T", g, c), kind, b)
                for part in range(2):
                    r = HI_HI_LO + part
                    for j in range(GH):
                        dst = qs[g][r:r + 1, j, c * HALF:(c + 1) * HALF].bitcast(F32).rearrange("o (t x) -> o t x", x=P)
                        sp.dma_start(dst, mrow[g][c][4 * j:4 * j + 4, part, :].bitcast(F32)).then_inc(s_mrow[g][c], 16)

            def step(kind, b):
                if kind == "prologue":
                    wait_used(sp, ("QK", 0, 0, 1), kind, b)
                    stack_rows(sp, 0, 0, (0,))
                    sp.wait_ge(s_part, 1)
                    stack_rows(sp, 0, 0, (2,))
                    wait_used(sp, ("QK", 1, 0, 1), kind, b)
                    stack_rows(sp, 0, 1, (0,))
                    sp.wait_ge(s_part, 2)
                    stack_rows(sp, 0, 1, (1,))
                    max_rows(0, 0, kind, b)
                    return
                if kind != "epilogue":
                    sp.wait_ge(s_wd, w_base(kind, b, "d"))
                    sp.wait_ge(s_part, 4 * b + 4)
                    for t in range(2):
                        stack_rows(sp, 1, t)
                if kind in ("first", "steady"):
                    sp.wait_ge(s_h, KT * (b + 1))
                    for k in range(KT):
                        sp.dma_start(xa[:, k, :], x_v[b + 1, :, k, :]).then_inc(s_x, 16)
                if kind == "first":
                    sp.dma_start(y[:, :, :], x_v[0]).then_inc(s_y, 16)
                if kind != "epilogue":
                    max_rows(0, 1, kind, b)
                if kind != "first":
                    wait_used(sp, ("QK1", 1), kind, b)
                    hi, lo = h[:, 0, :], h[:, 1, :]
                    for stack, p0, rows in ((qs1, 0, (hi, hi, lo)), (ks1, CH, (hi, lo, hi))):
                        for r, src in enumerate(rows):
                            sp.dma_start(stack[CH * r:CH * (r + 1), :].bitcast(F32), src[p0:p0 + CH, :]).then_inc(s_stack1, 16)
                if kind != "epilogue":
                    max_rows(1, 0, kind, b)
                if kind in ("first", "steady"):
                    sp.wait_ge(s_part, 4 * b + 6)
                    for t in range(2):
                        stack_rows(sp, 0, t)
                if kind != "first":
                    wait_used(sp, ("T1",), kind, b)
                    for part in range(2):
                        r = HI_HI_LO + part
                        dst = qs1[r:r + 1, :].bitcast(F32).rearrange("o (t x) -> o t x", x=P)
                        sp.dma_start(dst, mrow1[:, part, :].bitcast(F32)).then_inc(s_mrow1, 16)
                if kind != "epilogue":
                    max_rows(1, 1, kind, b)
                if kind != "first":
                    for c in range(4):
                        sp.wait_ge(s_done1, 4 * PIECES1 * (b - 1) + PIECES1 * (c + 1))
                        sp.dma_start(out_v[b - 1, :, :, c * QUARTER:(c + 1) * QUARTER],
                                     raw1[:, c, :, :]).then_inc(s_out[c], 16)
                if kind in ("steady", "last"):
                    sp.dma_start(y[:, :, :], x_v[b]).then_inc(s_y, 16)
                if kind in ("first", "steady"):
                    max_rows(0, 0, kind, b)

            run_steps(sp, step)
            for c in range(4):
                sp.wait_ge(s_out[c], 16 * (B + 1))

        @block.tensor
        def _(pe):
            mm = nc.tensor.matmul

            def scores_by_key(n, kind, b):
                layer, i = unit_use(n)
                for half in range(2):
                    at = 2 * n + half
                    before = at - ST_BANKS
                    while kind == "first" and before // 2 in range(L1_AT, L1_AT + L1_UNITS):
                        before -= ST_BANKS
                    if kind == "epilogue" and before < 2 * L1_AT:
                        pe.wait_ge(s_exp0, 2 * L0_UNITS * B)
                    elif before >= 0:
                        wait_exp(pe, before // 2, b, before % 2 + 1)
                    elif kind != "first":
                        pe.wait_ge(s_exp0, 2 * L0_UNITS * b + before + 1)
                    bank = st[:, at % ST_BANKS, :]
                    if layer:
                        c, part = i // 2, i % 2
                        if i == half == 0:
                            pe.wait_ge(s_mrow1, 32 * b)
                        for q in range(2):
                            s0 = (4 * part + 2 * half + q) * P
                            last = mm(bank[:, q * QUARTER:(q + 1) * QUARTER], ks1[0:ROWS, s0:s0 + P],
                                      qs1[0:ROWS, c * QUARTER:(c + 1) * QUARTER], start=True, stop=True)
                        last.then_inc(s_st1, 1)
                        continue
                    g, c, blk, pair = i // 32, i // 16 % 2, i % 16 // 2, i % 2
                    if i % 16 == half == 0:
                        pe.wait_ge(s_mrow[g][c], 128 * b + 128)
                    j = 2 * pair + half
                    mm(bank, ks[g][0:ROWS, j, blk * P:(blk + 1) * P], qs[g][0:ROWS, j, c * HALF:(c + 1) * HALF],
                       start=True, stop=True).then_inc(s_st0, 1)

            def product_l0(n, b):
                _, i = unit_use(n)
                g, blk = i // 32, i % 16 // 2
                wait_exp(pe, n, b)
                for j in range(GH):
                    last = mm(pv[CH * j:CH * (j + 1), :], vt[:, blk, g * P + CH * j:g * P + CH * (j + 1)],
                              probs[:, (n - 1 + j // 2) % PRING, (j % 2) * HALF:(j % 2 + 1) * HALF],
                              start=(blk == 0), stop=(blk == SB - 1), tile_position=(0, CH * j))
                last.then_inc(s_pv0, 1)

            def pv_free(ci, kind, b):
                if ci == L1_CHUNK and kind != "first":
                    pe.wait_ge(s_copy1, 4 * b)
                elif ci > 0 or kind != "first":
                    pe.wait_ge(s_copy0, 4 * b + ci)

            def product_l1(n, kind, b, between):
                _, i = unit_use(n)
                wait_exp(pe, n, b)
                if i == 0:
                    pe.wait_ge(s_copy0, 4 * B if kind == "epilogue" else 4 * b + L1_CHUNK)
                elif i % 2 == 0:
                    pe.wait_ge(s_copy1, 4 * (b - 1) + i // 2)
                for q in range(4):
                    for m in range(KT):
                        last = mm(pv[:, m * QUARTER:(m + 1) * QUARTER], vt1[:, 4 * (i % 2) + q, m * P:(m + 1) * P],
                                  probs[:, n % PRING, q * QUARTER:(q + 1) * QUARTER],
                                  start=(i % 2 == 0 and q == 0 and m == 0), stop=(i % 2 == 1 and q == 3),
                                  skip_group_check=True)
                    if q == 3:
                        last.then_inc(s_pv1, 1)
                    for e in between[q::4]:
                        fill_bank(e, kind, b)

            def fill_bank(e, kind, b):
                i = place[kind][e]
                if i >= WORK_BANKS:
                    wait_used(pe, banks[kind][i - WORK_BANKS], kind, b)
                elif kind != "prologue":
                    wait_used_before(pe, i, kind, b)
                bank = work[:, i % WORK_BANKS, :]
                what = e[0]
                if what == "M":
                    _, g, c, j, tb, half = e
                    if (j, tb, half) == (0, 0, 0) and c == 0:
                        pe.wait_ge(s_stack[g], 16 * STACK_DMAS * (b + (2 if g == 0 else 1)))
                    t0 = c * HALF + tb * P
                    last = mm(bank, qs[g][0:HI_HI_LO, j, t0:t0 + P], ks[g][0:HI_HI_LO, j, half * HALF:(half + 1) * HALF],
                              start=True, stop=True)
                elif what == "M1":
                    _, tb, half = e
                    if (tb, half) == (0, 0):
                        pe.wait_ge(s_stack1, 96 * b)
                    last = mm(bank, qs1[0:HI_HI_LO, tb * P:(tb + 1) * P], ks1[0:HI_HI_LO, half * HALF:(half + 1) * HALF],
                              start=True, stop=True)
                elif what == "T":
                    _, g, c = e
                    pe.wait_ge(s_mc[g][c], b + (2 if (g, c) == (0, 0) else 1))
                    last = nc.tensor.transpose(bank[0:16, 0:P], mcol[:, :], ident[:, :])
                elif what == "T1":
                    pe.wait_ge(s_mc1, b)
                    last = nc.tensor.transpose(bank[0:SB, 0:P], mcol1[:, :], ident[:, :])
                elif what == "SUM":
                    _, g, c = e
                    n_acc = (4 * (b - 1) if (g, c) == (1, 1) else 4 * b) + 2 * g + c + 1
                    pe.wait_ge(s_add0, 13 * n_acc)
                    pe.wait_ge(s_addv, n_acc)
                    for j in range(GH):
                        last = mm(bank[CH * j:CH * (j + 1), :], ones[:, 0:CH],
                                  acc[:, c, j // 2, (j % 2) * HALF:(j % 2 + 1) * HALF], start=True, stop=True,
                                  tile_position=(0, CH * j))
                elif what == "SUM1":
                    pe.wait_ge(s_add1, ADDS1 * (b - 1) + 3 * (e[1] + 1))
                    last = mm(bank[:, 0:QUARTER], ones[:, :], acc1[:, 0:QUARTER], start=True, stop=True)
                elif what == "P":
                    _, m, n = e
                    if m == 0:
                        pe.wait_ge(s_norm, PIECES * (4 * b - 1 + n))
                    for k in range(KT):
                        last = mm(bank, wproj[:, k, m * P:(m + 1) * P], attn[:, k, n * HALF:(n + 1) * HALF],
                                  start=(k == 0), stop=(k == KT - 1))
                elif what == "QK1":
                    n = e[1]
                    wait_used(pe, ("P", KT - 1, n), kind, b)
                    for k in range(KT):
                        last = mm(bank[0:2 * CH, :], wqk1[:, k, :], y[:, k, n * HALF:(n + 1) * HALF],
                                  start=(k == 0), stop=(k == KT - 1))
                elif what == "VT1":
                    for s in range(2):
                        blk = 2 * e[1] + s
                        for k in range(KT):
                            last = mm(bank[:, s * C:(s + 1) * C], y[:, k, blk * P:(blk + 1) * P], wv1[:, k, :],
                                      start=(k == 0), stop=(k == KT - 1))
                elif what == "PB":
                    for m in range(KT):
                        for k in range(KT):
                            last = mm(bank[:, m:m + 1], wproj[:, k, m * P:(m + 1) * P], qkvb[:, 4 + k:5 + k],
                                      start=(k == 0), stop=(k == KT - 1))
                elif what == "G1":
                    if kind == "prologue":
                        pe.wait_ge(s_norm_const, 16 * 4)
                    pe.wait_ge(s_stats, 6 * (b + 1) + 1)
                    last = mm(bank[:, 0:KT], gavg[:, :], mv[:, :, 0], start=True, stop=True)
                elif what == "G2":
                    wait_used(pe, ("G1",), kind, b)
                    last = mm(bank[:, 0:KT], gavg[:, :], vpd[:, :], start=True, stop=True)
                elif what == "QK":
                    _, t, g, n = e
                    if (t, g, n) == (0, 0, 0):
                        pe.wait_ge(s_h, KT * (b + 2))
                        if kind == "prologue":
                            pe.wait_ge(s_const, 16 * 8)
                            pe.wait_ge(s_ones, 4)
                    col = t * C + g * P
                    for k in range(KT):
                        last = mm(bank, wqkv[:, k, col:col + P], h[:, k, n * HALF:(n + 1) * HALF],
                                  start=(k == 0), stop=(k == KT - 1))
                elif what == "VT":
                    _, g, q = e
                    for s in range(4):
                        blk = 4 * q + s
                        for k in range(KT):
                            last = mm(bank[:, s * P:(s + 1) * P], h[:, k, blk * P:(blk + 1) * P],
                                      wqkv[:, k, 2 * C + g * P:2 * C + (g + 1) * P], start=(k == 0), stop=(k == KT - 1))
                last.then_inc(s_w, 1)

            def step(kind, b):
                units = slots_of(kind)
                for n, entries in enumerate(plans[kind]):
                    entries = [e for e in entries if e[0] not in NO_BANK]
                    if n in units:
                        scores_by_key(n, kind, b)
                    if L1_AT + 2 <= n < L1_AT + 2 + L1_UNITS and n - 2 in units:
                        if n == L1_AT + 2:
                            wait_used(pe, ("VT1", 3), kind, b)
                        product_l1(n - 2, kind, b, entries)
                        continue
                    for e in entries:
                        fill_bank(e, kind, b)
                    if n == 1 and kind not in ("prologue", "first"):
                        product_l0(SLOTS - 1, b - 1)
                    elif n % 2 and n - 3 in units and unit_use(n - 2)[0] == 0:
                        ci = unit_use(n - 2)[1] // 16
                        if unit_use(n - 2)[1] % 16 == 1:
                            pv_free(ci, kind, b)
                            if ci == 2:
                                wait_used(pe, ("VT", 1, 1), kind, b)
                            elif ci == 0 and kind == "first":
                                wait_used(pe, ("VT", 0, 1), "prologue", b - 1)
                        product_l0(n - 2, b)

            run_steps(pe, step)

        @block.scalar
        def _(act):
            def exponentials(n, kind, b):
                layer, i = unit_use(n)
                prev = n - PRING
                if kind == "first" and L1_AT <= prev < L1_AT + L1_UNITS:
                    prev -= -(-(prev - L1_AT + 1) // PRING) * PRING
                if kind == "epilogue" and n < L1_AT + PRING:
                    act.wait_ge(s_pv0, 32 * B)
                    act.wait_ge(s_addv, 4 * B)
                elif prev >= 0:
                    pl, pi = unit_use(prev)
                    if pl:
                        act.wait_ge(s_pv1, L1_UNITS * (b - 1) + pi + 1)
                        act.wait_ge(s_add1, ADDS1 * (b - 1) + 3 * (pi // 2) + 1)
                    else:
                        act.wait_ge(s_pv0, 32 * b + pi // 2 + 1)
                        wait_added(act, pi, b)
                elif kind != "first":
                    act.wait_ge(s_pv0, 32 * b + 1 + prev // 2)
                    wait_added(act, L0_UNITS + prev, b - 1)
                for half in range(2):
                    if layer:
                        act.wait_ge(s_st1, 2 * (L1_UNITS * (b - 1) + i) + half + 1)
                    else:
                        act.wait_ge(s_st0, 2 * (L0_UNITS * b + i) + half + 1)
                    nc.scalar.activation(probs[:, n % PRING, half * HALF:(half + 1) * HALF], st[:, (2 * n + half) % ST_BANKS, :],
                                         ACT.Exp).then_inc(s_exp1 if layer else s_exp0, 1)

            def use_bank(e, kind, b):
                i = place[kind][e]
                bank = work[:, i % WORK_BANKS, :]
                if e[0] == "QK" and e[3] == 0:
                    if kind == "prologue" and e == ("QK", 0, 0, 0):
                        act.wait_ge(s_scaled, 1)
                    if e[2] == 1 and kind == "prologue":
                        pass
                    elif e[1] == 0 and e[2] == 1:
                        act.wait_ge(s_stack[0], 16 * STACK_DMAS * (b + 2))
                    elif e[1] == 0 and kind != "prologue":
                        act.wait_ge(s_stack[1], 16 * STACK_DMAS * (b + 1))
                elif e == ("VT", 1, 0) and kind != "first":
                    act.wait_ge(s_pv0, 32 * b)
                elif e[0] == "SUM":
                    n = (4 * (b - 1) if e[1:] == (1, 1) else 4 * b) + 2 * e[1] + e[2]
                    if kind != "first" or e[1:] != (0, 0):
                        act.wait_ge(s_norm, PIECES * n)
                elif e[0] == "SUM1":
                    if e[1] >= 2:
                        act.wait_ge(s_done1, PIECES1 * (4 * (b - 1) + e[1] - 1))
                act.wait_ge(s_w, w_base(kind, b) + i + 1)
                if e[0] == "SUM":
                    last = nc.scalar.copy(rec[:, :], bank)
                elif e[0] == "SUM1":
                    last = nc.scalar.copy(rec1[:, e[1] % 2, :], bank[:, 0:QUARTER])
                elif e[0] == "QK":
                    _, t, g, n = e
                    if kind == "prologue" and g == 1:
                        dst = attn
                    else:
                        dst = part_lo
                        nc.scalar.activation(part_hi[:, t, n * HALF:(n + 1) * HALF], bank, ACT.Identity,
                                             bias=qkbs[:, 2 * t + g:2 * t + g + 1], scale=SCALE)
                    last = nc.scalar.activation(dst[:, t, n * HALF:(n + 1) * HALF], bank, ACT.Identity,
                                                bias=qkbs[:, 2 * t + g:2 * t + g + 1], scale=SCALE)
                elif e[0] == "VT":
                    _, g, q = e
                    last = nc.scalar.copy(vt[:, 4 * q:4 * q + 4, g * P:(g + 1) * P], bank.rearrange("p (s c) -> p s c", s=4))
                elif e[0] == "QK1":
                    n = e[1]
                    nc.scalar.copy(h[0:2 * CH, 0, n * HALF:(n + 1) * HALF].bitcast(F32R), bank[0:2 * CH, :]).then_inc(s_hi1, 1)
                    return
                else:
                    last = nc.scalar.copy(vt1[:, 2 * e[1]:2 * e[1] + 2, :], bank.rearrange("p (s c) -> p s c", s=2))
                last.then_inc(s_wa, 1)

            def step(kind, b):
                units = slots_of(kind)
                for n, entries in enumerate(plans[kind]):
                    if n in units:
                        exponentials(n, kind, b)
                    for e in entries:
                        if e[0] in SCALAR_USES or e[0] == "QK1":
                            use_bank(e, kind, b)
                        elif e[0] == "H":
                            act.wait_ge(s_stats, 6 * (b + 2))
                            if e[1] == 0 and kind != "prologue":
                                act.wait_ge(s_w, w_base(kind, b) + place[kind][("VT", 1, 1)] + 1)
                                if kind != "first":
                                    act.wait_ge(s_stack1, 96 * b)
                            nc.scalar.activation(h[:, e[1], :], xa[:, e[1], :], ACT.Identity, bias=aff_b[:, e[1]:e[1] + 1],
                                                 scale=aff_a[:, e[1]:e[1] + 1]).then_inc(s_h, 1)
                    if kind == "prologue":
                        continue
                    if L1_AT + 2 <= n < L1_AT + 2 + L1_UNITS and n % 2 and n - 2 in units:
                        c = (n - L1_AT - 3) // 2
                        act.wait_ge(s_pv1, L1_UNITS * (b - 1) + 2 * c + 2)
                        act.wait_ge(s_out[c], 16 * b)
                        nc.scalar.copy(raw1[:, c, :, :], pv[:, :].rearrange("p (m t) -> p m t", m=KT)).then_inc(s_copy1, 1)
                    ci = 3 if n == 1 and kind != "first" else {last_slot(c) + 2: c for c in range(3)}.get(n, -1)
                    if ci >= 0 and (kind != "epilogue" or ci == 3):
                        bb = b - 1 if ci == 3 else b
                        act.wait_ge(s_pv0, 32 * bb + 8 * (ci + 1))
                        if ci == 0 and kind != "first":
                            act.wait_ge(s_w, w_base(kind, b) + place[kind][("P", KT - 1, 1)] + 1)
                        nc.scalar.copy(attn[:, ci // 2, (ci % 2) * HALF:(ci % 2 + 1) * HALF], pv[:, :]).then_inc(s_copy0, 1)

            run_steps(act, step)

        @block.gpsimd
        def _(pool):
            pool.memset(ones[:, :], 1.0).then_inc(s_ones, 1)
            for i, rows in enumerate((ks[0][HI_HI_LO:ROWS, :, :], ks[1][HI_HI_LO:ROWS, :, :], ks1[HI_HI_LO:ROWS, :])):
                pool.wait_ge(s_ones, i + 1)
                pool.memset(rows.bitcast(F32), 1.0).then_inc(s_ones, 1)

            def step(kind, b):
                if kind == "prologue":
                    for t, r in ((0, 1), (1, 2)):
                        wait_used(pool, ("QK", t, 0, 1), kind, b)
                        stack_rows(pool, 0, t, (r,), s_soft)
                    pool.wait_ge(s_soft, 16 * 2 * GH)
                    pool.sem_inc(s_stack[0], 16 * 2 * GH)
                    return
                base = w_base(kind, b)
                for n in slots_of(kind):
                    layer, i = unit_use(n)
                    if layer:
                        c = i // 2
                        if i % 2 == 0:
                            continue
                        wait_exp(pool, n, b)
                        if c:
                            pool.wait_ge(s_w, base + place[kind][("SUM1", c - 1)] + 1)
                        a0 = ADDS1 * (b - 1) + 3 * c
                        pool.tensor_tensor(acc1, probs[:, (n - 1) % PRING, :], probs[:, n % PRING, :],
                                           ALU.add).then_inc(s_add1, 1)
                        pool.wait_ge(s_add1, a0 + 1)
                        pool.tensor_tensor(acc1[:, 0:HALF], acc1[:, 0:HALF], acc1[:, HALF:T], ALU.add).then_inc(s_add1, 1)
                        pool.wait_ge(s_add1, a0 + 2)
                        pool.tensor_tensor(acc1[:, 0:QUARTER], acc1[:, 0:QUARTER], acc1[:, QUARTER:HALF],
                                           ALU.add).then_inc(s_add1, 1)
                        continue
                    ci, blk, pair = i // 16, i % 16 // 2, i % 2
                    if blk == 0 or (blk, pair) == (SB - 1, 1):
                        continue
                    wait_exp(pool, n, b)
                    if blk == 1 and pair == 0:
                        if ci == 0 and kind != "first":
                            pool.wait_ge(s_w, base)
                        elif ci == 1 and kind != "first":
                            pool.wait_ge(s_w, base + place[kind][("SUM", 1, 1)] + 1)
                        elif ci == 3 and kind != "first":
                            pool.wait_ge(s_w, base + place[kind][("SUM1", 3)] + 1)
                        elif ci >= 2:
                            pool.wait_ge(s_w, base + place[kind][("SUM", 0, ci - 2)] + 1)
                    a = acc[:, ci % 2, pair, :]
                    if blk > 1:
                        wait_added(pool, i - 2, b)
                    first = probs[:, (n - 2) % PRING, :] if blk == 1 else a
                    pool.tensor_tensor(a, first, probs[:, n % PRING, :], ALU.add).then_inc(s_add0, 1)

            run_steps(pool, step)

        @block.vector
        def _(dve):
            def use_bank(e, kind, b):
                base = w_base(kind, b)
                i = place[kind][e]
                if e[0] == "M" and e[3:] == (0, 0, 0):
                    g, c = e[1:3]
                    if g == c == 0 and kind != "prologue":
                        dve.wait_ge(s_mc[1][1], b + 1)
                    elif (g, c) == (0, 1):
                        dve.wait_ge(s_mc[0][0], b + 2)
                    elif g:
                        dve.wait_ge(s_mc[g - 1 + c][1 - c], b + 1)
                dve.wait_ge(s_w, base + i + 1)
                bank = work[:, i % WORK_BANKS, :]
                what = e[0]
                if what == "M":
                    _, g, c, j, tb, half = e
                    last = dve.reduce_max(mpart[:, 4 * j + tb, half:half + 1], bank, AX.X)
                elif what == "M1":
                    _, tb, half = e
                    last = dve.reduce_max(mpart1[:, tb, half:half + 1], bank, AX.X)
                elif what in ("T", "T1"):
                    if what == "T":
                        _, g, c = e
                        ahead = 1 if (g, c) == (0, 0) else 0
                        rows, src, done, hi_done, n = (mrow[g][c], bank[0:16, 0:P], s_mrow[g][c], s_mhi[g][c], b + ahead)
                        if kind not in ("prologue", "first") or (kind == "first" and ahead):
                            dve.wait_ge(done, 128 * n)
                    else:
                        rows, src, hi_done, n = mrow1, bank[0:SB, 0:P], s_mhi1, b - 1
                    dve.tensor_scalar(rows[:, 0, :], src, -1.0, None, ALU.mult).then_inc(hi_done, 1)
                    dve.wait_ge(hi_done, n + 1)
                    last = dve.scalar_tensor_tensor(rows[:, 1, :], src, -1.0, rows[:, 0, :].bitcast(F32),
                                                    ALU.mult, ALU.subtract)
                elif what == "P":
                    _, m, n = e
                    if (m, n) == (0, 0):
                        dve.wait_ge(s_y, 16 * b)
                    yy = y[:, m, n * HALF:(n + 1) * HALF]
                    last = dve.scalar_tensor_tensor(yy, bank, outb[:, m:m + 1], yy, ALU.add, ALU.add)
                elif what == "QK1":
                    n = e[1]
                    src = bank[0:2 * CH, :]
                    hi = h[0:2 * CH, 0, n * HALF:(n + 1) * HALF]
                    dve.wait_ge(s_hi1, 2 * (b - 1) + n + 1)
                    last = dve.tensor_tensor(h[0:2 * CH, 1, n * HALF:(n + 1) * HALF].bitcast(F32R), src, hi, ALU.subtract)
                elif what == "PB":
                    dve.wait_ge(s_const, 16 * 8)
                    last = dve.tensor_tensor(outb[:, :], bank[:, 0:KT], projb[:, :], ALU.add)
                elif what == "G1":
                    n = 6 * (b + 1)
                    dve.tensor_copy(mu[:, :], bank[:, 0:KT])
                    dve.tensor_tensor(dev[:, :], mv[:, :, 0], bank[:, 0:KT], ALU.subtract).then_inc(s_stats, 1)
                    dve.wait_ge(s_stats, n + 2)
                    dve.tensor_tensor(dev2[:, :], dev[:, :], dev[:, :], ALU.mult).then_inc(s_stats, 1)
                    dve.wait_ge(s_stats, n + 3)
                    last = dve.tensor_tensor(vpd[:, :], dev2[:, :], mv[:, :, 1], ALU.add)
                elif what == "G2":
                    last = dve.tensor_scalar(var[:, :], bank[:, 0:KT], EPS, None, ALU.add)
                last.then_inc(s_wd, 1)

            def normalize(kind, b):
                base = w_base(kind, b)
                n = 6 * (b + 1)
                wait_used(dve, ("G2",), kind, b)
                k = (2 + 3 * NEWTON) * (b + 1)
                dve.tensor_scalar(half[:, :], var[:, :].bitcast(I32), 1, None, ALU.logical_shift_right).then_inc(s_rsqrt, 1)
                dve.wait_ge(s_rsqrt, k + 1)
                dve.tensor_scalar(rstd[:, :].bitcast(I32), half[:, :], -1.0, float(0x5F3759DF), ALU.mult,
                                  ALU.add).then_inc(s_rsqrt, 1)
                for i in range(NEWTON):
                    dve.wait_ge(s_rsqrt, k + 2 + 3 * i)
                    dve.scalar_tensor_tensor(dev[:, :], rstd[:, :], -0.5, rstd[:, :], ALU.mult, ALU.mult).then_inc(s_rsqrt, 1)
                    dve.wait_ge(s_rsqrt, k + 3 + 3 * i)
                    dve.tensor_tensor(dev2[:, :], dev[:, :], var[:, :], ALU.mult).then_inc(s_rsqrt, 1)
                    dve.wait_ge(s_rsqrt, k + 4 + 3 * i)
                    dve.scalar_tensor_tensor(rstd[:, :], dev2[:, :], 1.5, rstd[:, :], ALU.add, ALU.mult).then_inc(s_rsqrt, 1)
                dve.wait_ge(s_rsqrt, k + 2 + 3 * NEWTON)
                dve.tensor_tensor(aff_a[:, :], rstd[:, :], gnw[:, :], ALU.mult).then_inc(s_stats, 1)
                dve.wait_ge(s_stats, n + 4)
                dve.tensor_tensor(mua[:, :], mu[:, :], aff_a[:, :], ALU.mult).then_inc(s_stats, 1)
                dve.wait_ge(s_stats, n + 5)
                dve.tensor_tensor(aff_b[:, :], gnb[:, :], mua[:, :], ALU.subtract).then_inc(s_stats, 1)
                dve.wait_ge(s_stats, n + 6)

            def own_step(e, kind, b):
                if e[0] == "HL":
                    _, t, g = e
                    wait_used(dve, ("QK", t, g, 1), kind, b)
                    if g == 0 and kind != "prologue":
                        dve.wait_ge(s_st0, 2 * (L0_UNITS * b + 32))
                    src = part_lo
                    if kind == "prologue" and g == 1:
                        src = attn
                        dve.wait_ge(s_stack[0], 16 * STACK_DMAS)
                        dve.tensor_copy(part_hi[:, t, :], src[:, t, :]).then_inc(s_hi, 1)
                        dve.wait_ge(s_hi, t + 1)
                    dve.tensor_tensor(part_lo[:, t, :].bitcast(F32R), src[:, t, :], part_hi[:, t, :].bitcast(F32),
                                      ALU.subtract).then_inc(s_part, 1)
                elif e[0] == "R":
                    _, g, c, p = e
                    n = (4 * (b - 1) if (g, c) == (1, 1) else 4 * b) + 2 * g + c
                    if p == 0:
                        wait_used(dve, ("SUM", g, c), kind, b)
                        dve.wait_ge(s_copy0, n + 1)
                    r = rec[:, p * PIECE:(p + 1) * PIECE]
                    dve.reciprocal(r, r).then_inc(s_rec, 1)
                    dve.wait_ge(s_rec, PIECES * n + p + 1)
                    a = attn[:, g, c * HALF + p * PIECE:c * HALF + (p + 1) * PIECE]
                    dve.tensor_tensor(a, a, r, ALU.mult).then_inc(s_norm, 1)
                elif e[0] == "R1":
                    _, c, p = e
                    n = PIECES1 * (4 * (b - 1) + c) + p
                    if p == 0:
                        wait_used(dve, ("SUM1", c), kind, b)
                        dve.wait_ge(s_copy1, 4 * (b - 1) + c + 1)
                    r = rec1[:, c % 2, p * PIECE:(p + 1) * PIECE]
                    dve.reciprocal(r, r).then_inc(s_rec1, 1)
                    dve.wait_ge(s_rec1, n + 1)
                    a = raw1[:, c, :, p * PIECE:(p + 1) * PIECE]
                    for m in range(KT):
                        dve.scalar_tensor_tensor(a[:, m, :], a[:, m, :], gam[:, 0:1], r, ALU.mult, ALU.mult).then_inc(s_sc1, 1)
                    dve.wait_ge(s_sc1, 2 * n + 2)
                    t0 = c * QUARTER + p * PIECE
                    dve.tensor_tensor(a, a, y[:, :, t0:t0 + PIECE], ALU.add).then_inc(s_done1, 1)
                elif e[0] == "BN":
                    k = e[1]
                    if k == 0:
                        dve.wait_ge(s_x, 32 * (b + 2))
                    for n in range(2):
                        s = dve.bn_stats(bst[:, k, n, :], xa[:, k, n * HALF:(n + 1) * HALF])
                    s.then_inc(s_bn, 1)
                elif e[0] == "AGG":
                    dve.wait_ge(s_bn, KT * (b + 2))
                    dve.memset(carry[:, :], 0.0)
                    dve.bn_aggr(mv[:, 0, :], bst[:, 0, :, :])
                    dve.bn_aggr(mv[:, 1, :], bst[:, 1, :, :]).then_inc(s_stats, 1)
                elif e[0] == "NORM":
                    normalize(kind, b)
                elif e[0] == "A":
                    ci, pair = e[1], 1
                    bb = b - 1 if ci == 3 else b
                    i = 16 * ci + 14 + pair
                    dve.wait_ge(s_exp0, 2 * (L0_UNITS * bb + i + 1))
                    wait_added(dve, i - 2, bb)
                    n = last_slot(ci) - 1 + pair
                    a = acc[:, ci % 2, pair, :]
                    dve.tensor_tensor(a, a, probs[:, n % PRING, :], ALU.add).then_inc(s_addv, 1)
                elif e[0] == "MC":
                    _, g, c = e
                    wait_used(dve, ("M", g, c, GH - 1, 3, 1), kind, b)
                    dve.tensor_tensor(mcol[:, :], mpart[:, :, 0], mpart[:, :, 1], ALU.max).then_inc(s_mc[g][c], 1)
                else:
                    wait_used(dve, ("M1", SB - 1, 1), kind, b)
                    dve.tensor_tensor(mcol1[:, :], mpart1[:, :, 0], mpart1[:, :, 1], ALU.max).then_inc(s_mc1, 1)

            def step(kind, b):
                for entries in plans[kind]:
                    for e in entries:
                        if e[0] == "H":
                            continue
                        if e[0] in NO_BANK:
                            own_step(e, kind, b)
                        elif e[0] not in SCALAR_USES:
                            use_bank(e, kind, b)

            s_bn = sem("s_bn")
            dve.wait_ge(s_norm_const, 16 * 4)
            dve.tensor_scalar(qkbs[:, :], qkvb[:, 0:4], SCALE, None, ALU.mult).then_inc(s_scaled, 1)
            run_steps(dve, step)


def kernel(x, L0_conv_gn_w, L0_conv_gn_b, L0_conv_qkv_w, L0_conv_qkv_b, L0_conv_proj_w, L0_conv_proj_b,
           L1_conv_Wq, L1_conv_Wk, L1_conv_Wv, L1_conv_gamma):
    import numpy as np
    import concourse.bacc as bacc
    from concourse.bass_utils import run_bass_kernel_spmd

    def columns(v):
        return np.ascontiguousarray(np.asarray(v).reshape(-1, P).T)

    def parts_first(w):
        w = np.asarray(w)
        return np.swapaxes(w.reshape(HEADS, 3, CH, -1), 0, 1).reshape(3 * C, -1)

    x = np.asarray(x)
    group = np.arange(P) // (C // 32)
    arrays = {
        "x": np.ascontiguousarray(x.reshape(B, C, T)),
        "qkv_wT": np.ascontiguousarray(parts_first(L0_conv_qkv_w).T),
        "qkv_b": columns(parts_first(L0_conv_qkv_b).reshape(-1)),
        "gn_w": columns(L0_conv_gn_w),
        "gn_b": columns(L0_conv_gn_b),
        "proj_wT": np.ascontiguousarray(np.asarray(L0_conv_proj_w).T),
        "proj_b": columns(L0_conv_proj_b),
        "wqT": np.ascontiguousarray(np.asarray(L1_conv_Wq).T),
        "wkT": np.ascontiguousarray(np.asarray(L1_conv_Wk).T),
        "wvT": np.ascontiguousarray(np.asarray(L1_conv_Wv).T),
        "gamma": np.ascontiguousarray(np.broadcast_to(np.asarray(L1_conv_gamma).reshape(1, 1), (P, 1))),
        "ident": np.eye(P, dtype=np.float32),
        "gavg": ((group[:, None] == group[None, :]) / (C // 32)).astype(np.float32),
    }
    nc = bacc.Bacc("TRN2", target_bir_lowering=False, num_devices=1)
    args = [nc.dram_tensor(f"in_{k}", a.shape, mybir.dt.from_np(a.dtype), kind="ExternalInput").ap()
            for k, a in arrays.items()]
    out = nc.dram_tensor("out_0", (B, C, T), F32, kind="ExternalOutput").ap()
    attention(nc, *args, out)
    r = run_bass_kernel_spmd(nc, [{f"in_{k}": a for k, a in arrays.items()}], core_ids=[0])
    return r.results[0]["out_0"].reshape(x.shape)
```
